# Optimizing a Trainium2 kernel written in Bass

```python
import numpy as np
import jax
import jax.numpy as jnp

def _softmax(x, axis=-1):
    return jax.nn.softmax(x, axis=axis)

def _gelu(x):
    return jax.nn.gelu(x, approximate=True)

def _silu(x):
    return jax.nn.silu(x)

def _sigmoid(x):
    return jax.nn.sigmoid(x)

def _layernorm(x, axis=-1, eps=1e-05):
    m = jnp.mean(x, axis=axis, keepdims=True)
    v = jnp.var(x, axis=axis, keepdims=True)
    return (x - m) / jnp.sqrt(v + eps)

def _scatter_add(tgt, idx, src, axis=0):
    return tgt.at[idx].add(src)

def _segment_sum(src, seg, n):
    return jax.ops.segment_sum(src, seg, n)
kernel_name = 'mk_adj_preln_d1_adj_r2_91aaea'

def setup_inputs(seed: int=0):
    np.random.seed(seed)
    _w = jnp.asarray

    def _rec_inputs():
        import jax
        import jax.numpy as jnp
        _gk = jax.random.key(seed)
        x = 7.22e-05 + 1 * jax.random.normal(jax.random.fold_in(_gk, 1), (32, 256, 128), jnp.float32)
        _w = (1.0 + jnp.arange(256, dtype=jnp.float32)) ** (-0.5)
        _w = _w / _w.mean()
        _pij = jnp.clip(0.0078125 * _w[:, None] * _w[None, :], 0.0, 1.0)
        _a = jax.random.uniform(jax.random.fold_in(_gk, 2), (32, 256, 256)) < _pij
        _a = jnp.logical_or(_a, jnp.swapaxes(_a, -1, -2))
        _a = jnp.logical_or(_a, jnp.eye(256, dtype=bool))
        _af = _a.astype(jnp.float32)
        adj = _af
        return (x, adj)
    x, adj = _rec_inputs()

    def _L0_gnn_setup():
        import jax, jax.numpy as jnp
        import numpy as np
        from jax import lax
        DIM = 128
        EPS = 1e-05

        def _bn(h, g, b, m, v):
            scale = g / jnp.sqrt(v + EPS)
            return h * scale[None, :, None] + (b - m * scale)[None, :, None]

        def _conv1d(h, w, pad):
            return lax.conv_general_dilated(h, w, window_strides=(1,), padding=[(pad, pad)], dimension_numbers=('NCH', 'OIH', 'NCH'))
        key = jax.random.key(seed)
        ks = jax.random.split(key, 16)
        bs, n, d = (16, 1024, DIM)
        s = 0.05
        return {'x': jax.random.normal(ks[0], (bs, n, d), jnp.float32), 'mask': jnp.ones((bs, n, n), jnp.float32), 'w_se': jax.random.normal(ks[1], (3, d), jnp.float32) * s, 'b_se': jnp.zeros((3,), jnp.float32), 'conv1_w': jax.random.normal(ks[2], (d, d, 1), jnp.float32) * s, 'bn1_g': jnp.ones((d,), jnp.float32), 'bn1_b': jnp.zeros((d,), jnp.float32), 'bn1_m': jnp.zeros((d,), jnp.float32), 'bn1_v': jnp.ones((d,), jnp.float32), 'conv2_w': jax.random.normal(ks[3], (d, d, 17), jnp.float32) * s, 'bn2_g': jnp.ones((d,), jnp.float32), 'bn2_b': jnp.zeros((d,), jnp.float32), 'bn2_m': jnp.zeros((d,), jnp.float32), 'bn2_v': jnp.ones((d,), jnp.float32), 'w_msg': jax.random.normal(ks[4], (d, d), jnp.float32) * s, 'b_msg': jnp.zeros((d,), jnp.float32), 'w_ih': jax.random.normal(ks[5], (3 * d, 2 * d), jnp.float32) * s, 'b_ih': jnp.zeros((3 * d,), jnp.float32), 'w_hh': jax.random.normal(ks[6], (3 * d, d), jnp.float32) * s, 'b_hh': jnp.zeros((3 * d,), jnp.float32)}
    _L0_gnn_all = _L0_gnn_setup()
    _L0_gnn_in = {k: v for k, v in _L0_gnn_all.items() if k in ('w_se', 'b_se', 'conv1_w', 'bn1_g', 'bn1_b', 'bn1_m', 'bn1_v', 'conv2_w', 'bn2_g', 'bn2_b', 'bn2_m', 'bn2_v', 'w_msg', 'b_msg', 'w_ih', 'b_ih', 'w_hh', 'b_hh')}
    del _L0_gnn_all
    return {'x': x, 'adj': adj, 'L0_gnn_w_se': _L0_gnn_in['w_se'], 'L0_gnn_b_se': _L0_gnn_in['b_se'], 'L0_gnn_conv1_w': _L0_gnn_in['conv1_w'], 'L0_gnn_bn1_g': _L0_gnn_in['bn1_g'], 'L0_gnn_bn1_b': _L0_gnn_in['bn1_b'], 'L0_gnn_bn1_m': _L0_gnn_in['bn1_m'], 'L0_gnn_bn1_v': _L0_gnn_in['bn1_v'], 'L0_gnn_conv2_w': _L0_gnn_in['conv2_w'], 'L0_gnn_bn2_g': _L0_gnn_in['bn2_g'], 'L0_gnn_bn2_b': _L0_gnn_in['bn2_b'], 'L0_gnn_bn2_m': _L0_gnn_in['bn2_m'], 'L0_gnn_bn2_v': _L0_gnn_in['bn2_v'], 'L0_gnn_w_msg': _L0_gnn_in['w_msg'], 'L0_gnn_b_msg': _L0_gnn_in['b_msg'], 'L0_gnn_w_ih': _L0_gnn_in['w_ih'], 'L0_gnn_b_ih': _L0_gnn_in['b_ih'], 'L0_gnn_w_hh': _L0_gnn_in['w_hh'], 'L0_gnn_b_hh': _L0_gnn_in['b_hh']}

def reference(x, adj, L0_gnn_w_se, L0_gnn_b_se, L0_gnn_conv1_w, L0_gnn_bn1_g, L0_gnn_bn1_b, L0_gnn_bn1_m, L0_gnn_bn1_v, L0_gnn_conv2_w, L0_gnn_bn2_g, L0_gnn_bn2_b, L0_gnn_bn2_m, L0_gnn_bn2_v, L0_gnn_w_msg, L0_gnn_b_msg, L0_gnn_w_ih, L0_gnn_b_ih, L0_gnn_w_hh, L0_gnn_b_hh):
    import jax
    import jax.numpy as jnp

    def _L0_gnn_ref(x, mask, w_se, b_se, conv1_w, bn1_g, bn1_b, bn1_m, bn1_v, conv2_w, bn2_g, bn2_b, bn2_m, bn2_v, w_msg, b_msg, w_ih, b_ih, w_hh, b_hh):
        import jax, jax.numpy as jnp
        import numpy as np
        from jax import lax
        DIM = 128
        EPS = 1e-05

        def _bn(h, g, b, m, v):
            scale = g / jnp.sqrt(v + EPS)
            return h * scale[None, :, None] + (b - m * scale)[None, :, None]

        def _conv1d(h, w, pad):
            return lax.conv_general_dilated(h, w, window_strides=(1,), padding=[(pad, pad)], dimension_numbers=('NCH', 'OIH', 'NCH'))
        d = x.shape[-1]
        xc = jnp.transpose(x, (0, 2, 1))
        h = _bn(_conv1d(xc, conv1_w, 0), bn1_g, bn1_b, bn1_m, bn1_v)
        h = jax.nn.relu(h)
        h = _bn(_conv1d(h, conv2_w, 8), bn2_g, bn2_b, bn2_m, bn2_v)
        x_conv = jnp.transpose(jax.nn.relu(h + xc), (0, 2, 1))
        s = x @ w_se.T + b_se
        sq = jnp.sum(s * s, axis=-1)
        dist = sq[:, :, None] + sq[:, None, :] - 2.0 * jnp.einsum('bnd,bmd->bnm', s, s)
        A = jnp.exp(-dist) * mask
        msg = jax.nn.relu(x @ w_msg.T + b_msg)
        x_nmp = jnp.einsum('bnm,bmd->bnd', A, msg)
        x_in = jnp.concatenate([x_conv, x_nmp], axis=-1)
        gi = x_in @ w_ih.T + b_ih
        gh = x @ w_hh.T + b_hh
        gi_r, gi_z, gi_n = (gi[..., :d], gi[..., d:2 * d], gi[..., 2 * d:])
        gh_r, gh_z, gh_n = (gh[..., :d], gh[..., d:2 * d], gh[..., 2 * d:])
        r = jax.nn.sigmoid(gi_r + gh_r)
        z = jax.nn.sigmoid(gi_z + gh_z)
        nn_ = jnp.tanh(gi_n + r * gh_n)
        return (1.0 - z) * nn_ + z * x
    h = jnp.maximum(_layernorm(x, axis=-1), 0.0)
    x = x + _L0_gnn_ref(h, adj, L0_gnn_w_se, L0_gnn_b_se, L0_gnn_conv1_w, L0_gnn_bn1_g, L0_gnn_bn1_b, L0_gnn_bn1_m, L0_gnn_bn1_v, L0_gnn_conv2_w, L0_gnn_bn2_g, L0_gnn_bn2_b, L0_gnn_bn2_m, L0_gnn_bn2_v, L0_gnn_w_msg, L0_gnn_b_msg, L0_gnn_w_ih, L0_gnn_b_ih, L0_gnn_w_hh, L0_gnn_b_hh)
    return x

_drawn_inputs = setup_inputs


def setup_inputs(seed=0):
    import zlib

    import numpy as np

    out = dict(_drawn_inputs(seed))
    spreads = {'L0_gnn_b_se': (0.0, 0.8),
     'L0_gnn_bn1_g': (1.0, 0.6),
     'L0_gnn_bn1_b': (0.0, 0.344),
     'L0_gnn_bn1_m': (0.0, 0.338),
     'L0_gnn_bn1_v': (1.0, 0.6),
     'L0_gnn_bn2_g': (1.0, 0.6),
     'L0_gnn_bn2_b': (0.0, 0.531),
     'L0_gnn_bn2_m': (0.0, 0.512),
     'L0_gnn_bn2_v': (1.0, 0.6),
     'L0_gnn_b_msg': (0.0, 0.1),
     'L0_gnn_b_ih': (0.0, 0.1),
     'L0_gnn_b_hh': (0.0, 0.341)}
    factors = {}
    for name, (base, spread) in spreads.items():
        noise = np.random.default_rng([zlib.crc32(name.encode()), seed]).standard_normal(out[name].shape)
        drawn = base * np.exp(spread * noise) if base else spread * noise
        out[name] = jnp.asarray(drawn.astype(out[name].dtype))
    for name, factor in factors.items():
        out[name] = (out[name] * factor).astype(out[name].dtype)
    return out
```

```python
import concourse.bass as bass
from concourse import mybir
from contextlib import ExitStack

P = 128
N_BATCH, N_NODE = 32, 256
STEP_B = 4
STEP_TOK = STEP_B * N_NODE
STEPS = N_BATCH // STEP_B
TILES = STEP_TOK // P
HALF = 512
MT = N_NODE // P
TAPS, PAD = 17, 8
ROW = N_NODE + 2 * PAD
MSGW = P + 4
EPS = 1e-5
(V_G1, V_B1, V_M1, V_V1, V_G2, V_B2, V_M2, V_V2, V_IR, V_IZ, V_IN, V_HR, V_HZ, V_HN) = range(14)
NVEC = 14


def gnn_layer(nc, x_tok, x_chan, mask_t, vec_col, vec_row, msg_row, w1, w2, wg, wm, out):
    f32, f32r = mybir.dt.float32, mybir.dt.float32r
    ALU, ACT, AX = mybir.AluOpType, mybir.ActivationFunctionType, mybir.AxisListType
    ctx = ExitStack()
    with ctx:
        def sb(name, shape, dt=f32):
            return ctx.enter_context(nc.sbuf_tensor(name, shape, dt))

        def sem(name):
            return ctx.enter_context(nc.semaphore(name))

        vcol = sb("vcol", [P, NVEC])
        vrow = sb("vrow", [P, 3, P])
        mrow = sb("mrow", [P, 3 * MSGW])
        w1_raw = sb("w1_raw", [P, P])
        w2_raw = sb("w2_raw", [P, TAPS, P])
        wg_raw = sb("wg_raw", [P, 3, 3 * P])
        wm_sb = sb("wm_sb", [P, MSGW])
        w1_hi, w1_lo = sb("w1_hi", [P, P], f32r), sb("w1_lo", [P, P], f32r)
        w2_hi, w2_lo = sb("w2_hi", [P, TAPS, P], f32r), sb("w2_lo", [P, TAPS, P], f32r)
        wg_hi, wg_lo = sb("wg_hi", [P, 3, 3 * P], f32r), sb("wg_lo", [P, 3, 3 * P], f32r)
        ident = sb("ident", [P, P])
        ident_r = sb("ident_r", [P, P], f32r)
        ones = sb("ones", [P, HALF], f32r)
        ones32 = sb("ones32", [P, HALF])
        zeros32 = sb("zeros32", [P, 2 * HALF])
        scale_r = sb("scale_r", [P, P])
        scale_c = sb("scale_c", [P, 2])
        bias_c = sb("bias_c", [P, 5])
        tmp_c = sb("tmp_c", [P, 2])
        minus_half = sb("minus_half", [P, P])
        minus_one, quarter = sb("minus_one", [P, TILES]), sb("quarter", [P, TILES])
        ghn_row = sb("ghn_row", [P, P])
        ghn_hi = sb("ghn_hi", [P, P], f32r)
        mrow_hi = sb("mrow_hi", [P, 3 * MSGW], f32r)
        bias_ghn = sb("bias_ghn", [P, P], f32r)
        bias_msg = sb("bias_msg", [P, 3 * MSGW], f32r)
        xt = [sb(f"xt{k}", [P, TILES, P]) for k in range(2)]
        stats = sb("stats", [P, TILES, 6])
        mo_sum, mo_dif, mo_dev, mo_sq, mean, rstd = (sb(n, [P, TILES, 1]) for n in ("mo_sum", "mo_dif", "mo_dev", "mo_sq", "mean", "rstd"))
        xn = sb("xn", [P, TILES, P])
        h = [sb(f"h{k}", [P, STEP_TOK]) for k in range(2)]
        h_hi = [sb(f"h_hi{k}", [P, STEP_TOK], f32r) for k in range(2)]
        h_lo = [sb(f"h_lo{k}", [P, STEP_TOK], f32r) for k in range(2)]
        c1 = sb("c1", [P, STEP_B, N_NODE])
        c1_hi = [sb(f"c1_hi{k}", [P, STEP_B, ROW], f32r) for k in range(2)]
        c1_lo = [sb(f"c1_lo{k}", [P, STEP_B, ROW], f32r) for k in range(2)]
        msg = sb("msg", [P, TILES, P])
        se = sb("se", [P, TILES, 3])
        se_hi = sb("se_hi", [P, TILES, 3], f32r)
        sq_el = sb("sq_el", [P, TILES, 3])
        sq, sq_a = sb("sq", [P, TILES, 1]), sb("sq_a", [P, TILES, 1])
        nsq_hi = sb("nsq_hi", [P, TILES, 1], f32r)
        se_parts = sb("se_parts", [P, TILES, 2, 3])
        feat = sb("feat", [P, TILES, P])
        f_nb = sb("f_nb", [P, STEP_TOK], f32r)
        f_nd = sb("f_nd", [P, STEP_TOK], f32r)
        mask = [sb(f"mask{k}", [P, STEP_B, HALF]) for k in range(2)]
        aff = sb("aff", [P, STEP_B, HALF])
        agg_hi, agg_lo = sb("agg_hi", [P, STEP_TOK], f32r), sb("agg_lo", [P, STEP_TOK], f32r)
        xc = sb("xc", [P, STEP_TOK])
        xc_hi, xc_lo = sb("xc_hi", [P, STEP_TOK], f32r), sb("xc_lo", [P, STEP_TOK], f32r)
        res = [sb(f"res{k}", [P, STEP_TOK]) for k in range(2)]
        tr = [sb(f"tr{k}", [P, HALF]) for k in range(2)]
        tz = [sb(f"tz{k}", [P, HALF]) for k in range(2)]
        rg = pre = tr
        cand = [sb(f"cand{k}", [P, HALF]) for k in range(2)]
        dif = [sb(f"dif{k}", [P, HALF]) for k in range(2)]
        zd = upd = dif
        y = [sb(f"y{k}", [P, HALF]) for k in range(2)]
        bank = [ctx.enter_context(nc.psum_tensor(f"bank{k}", [P, HALF], f32)) for k in range(8)]
        B_AGG = (0, 4)
        B_C2 = (1, 0)
        B_FRONT = (2, 3)
        B_MSG = (4, 5, 6)
        B_R, B_Z, B_GN, B_IN = 4, 5, 6, 7
        B_DIST = (2, 3, 1, 0)
        MSG_LOTS = [(0, 3), (3, 3), (6, 2)]

        s_vec, s_row, s_w1, s_w2, s_wg, s_wm = (sem(n) for n in ("s_vec", "s_row", "s_w1", "s_w2", "s_wg", "s_wm"))
        s_x = [sem(f"s_x{k}") for k in range(2)]
        s_res = [sem(f"s_res{k}") for k in range(2)]
        s_mask = [sem(f"s_mask{k}") for k in range(2)]
        s_out = [sem(f"s_out{k}") for k in range(2)]
        pool_set = sem("pool_set")
        pool_pow = sem("pool_pow")
        dve_set = sem("dve_set")
        w_ready = sem("w_ready")
        st_done, pm, xn_done = sem("st_done"), sem("pm"), sem("xn_done")
        tr_done = sem("tr_done")
        h_done, hh_done, hl_done = sem("h_done"), sem("hh_done"), sem("hl_done")
        c1_mm, c1_act, c1h_done, c1l_done = sem("c1_mm"), sem("c1_act"), sem("c1h_done"), sem("c1l_done")
        ms_mm, ms_act, se_act = sem("ms_mm"), sem("ms_act"), sem("se_act")
        pf = sem("pf")
        ft_mm, ft_act = sem("ft_mm"), sem("ft_act")
        di_mm, exp_done, aff_done = sem("di_mm"), sem("exp_done"), sem("aff_done")
        ag_mm, agh_done, agl_done = sem("ag_mm"), sem("agh_done"), sem("agl_done")
        c2_mm, xc_done, xch_done, xcl_done = sem("c2_mm"), sem("xc_done"), sem("xch_done"), sem("xcl_done")
        g_mm = sem("g_mm")
        tr_act, tz_act, rg_done, pre_done, cand_done = (sem(n) for n in ("tr_act", "tz_act", "rg_done", "pre_done", "cand_done"))
        dif_done, zd_done, upd_done, y_done = sem("dif_done"), sem("zd_done"), sem("upd_done"), sem("y_done")
        PF, PM = 6, 5

        class Step:
            def __init__(self, j, c):
                self.j, self.c = j, c

            def __add__(self, d):
                return Step(self.j, self.c + d)

            def par(self):
                return self.c % 2

            def n(self):
                return self.j * 2 + self.c

            def after(self, per, k):
                return self.j * (2 * per) + (self.c * per + k)

            def load(self):
                return self.j * 16 + 16 * (self.c // 2 + 1)

        def steps(eng, body):
            body(Step(0, 0), True, True)
            body(Step(0, 1), True, True)
            with eng.Fori(1, (STEPS - 2) // 2) as j:
                body(Step(j, 0), True, True)
                body(Step(j, 1), True, True)
            body(Step((STEPS - 2) // 2, 0), True, False)
            body(Step((STEPS - 2) // 2, 1), False, False)

        def past(eng, semaphore, value):
            if not isinstance(value, int) or value > 0:
                eng.wait_ge(semaphore, value)

        def halves(k):
            return slice(k * HALF, (k + 1) * HALF)

        block = ctx.enter_context(nc.Block())

        @block.sync
        def _(sp):
            def load_x(s):
                sp.dma_start(xt[s.par()][:], x_tok[bass.ds(s.n(), 1)].rearrange("o p t c -> p (o t) c")).then_inc(s_x[s.par()], 16)

            def load_mask(s):
                sp.dma_start(mask[s.par()][:], mask_t[bass.ds(s.n(), 1)].rearrange("o p b n -> p (o b) n")).then_inc(s_mask[s.par()], 16)

            def load_res(s):
                sp.dma_start(res[s.par()][:], x_chan[bass.ds(s.n(), 1)].rearrange("o p t -> p (o t)")).then_inc(s_res[s.par()], 16)

            first = Step(0, 0)
            load_x(first)
            sp.dma_start(vcol[:], vec_col).then_inc(s_vec, 16)
            sp.dma_start(vrow[:].rearrange("p v c -> p (v c)"), vec_row.to_broadcast([P, 3 * P])).then_inc(s_row, 16)
            sp.dma_start(w1_raw[:], w1).then_inc(s_w1, 16)
            sp.dma_start(mrow[:], msg_row.to_broadcast([P, 3 * MSGW])).then_inc(s_row, 16)
            sp.dma_start(wm_sb[:], wm).then_inc(s_wm, 16)
            load_mask(first)
            load_x(first + 1)
            sp.dma_start(w2_raw[:], w2).then_inc(s_w2, 16)
            sp.dma_start(wg_raw[:], wg).then_inc(s_wg, 16)
            load_res(first)
            load_mask(first + 1)

            def body(i, front, norm):
                if front:
                    past(sp, y_done, i.after(2, 0))
                    load_res(i + 1)
                if norm:
                    sp.wait_ge(xn_done, i.after(1, 1))
                    load_x(i + 2)
                    sp.wait_ge(aff_done, i.after(STEP_B, STEP_B))
                    load_mask(i + 2)
                for k in range(2):
                    sp.wait_ge(y_done, i.after(2, k + 1))
                    sp.dma_start(out[bass.ds(i.n(), 1), :, halves(k)].rearrange("o p t -> p (o t)"), y[k][:]).then_inc(s_out[k], 16)

            steps(sp, body)
            for k in range(2):
                sp.wait_ge(s_out[k], 16 * STEPS)

        @block.gpsimd
        def _(pool):
            chain = [0]

            def link(ins):
                chain[0] += 1
                ins.then_inc(pool_set, 1)
                pool.wait_ge(pool_set, chain[0])

            pool.memset(zeros32[:], 0.0).then_inc(pool_set, 1)
            pool.memset(ones32[:], 1.0).then_inc(pool_set, 1)
            pool.memset(minus_half[:], -0.5).then_inc(pool_set, 1)
            pool.memset(minus_one[:], -1.0).then_inc(pool_set, 1)
            pool.memset(quarter[:], 0.25).then_inc(pool_set, 1)
            chain[0] = 5
            one3 = ones32[:, 0:3 * TILES].rearrange("p (t c) -> p t c", c=3)
            minus_one1, quarter1 = minus_one[:].unsqueeze(2), quarter[:].unsqueeze(2)
            link(pool.memset(ident[:], 0.0))
            link(pool.affine_select(out=ident[:], in_=ident[:], compare_op=ALU.not_equal, fill=1.0, base=0,
                                    pattern=[[-1, P]], channel_multiplier=1))
            link(pool.memset(feat[:], 0.0))
            link(pool.memset(feat[:, :, 12:14], 1.0))
            link(pool.memset(feat[:, :, 46:48], 1.0))

            def factors(s):
                g = [0]

                def done(ins):
                    g[0] += 1
                    ins.then_inc(pf, 1)
                    pool.wait_ge(pf, s.after(PF, g[0]))
                past(pool, ft_mm, s.after(2, 0))
                pool.wait_ge(se_act, s.after(3, 3))
                pool.tensor_tensor(se_hi[:], se[:], one3, ALU.mult)
                done(pool.tensor_tensor(sq_el[:], se[:], se[:], ALU.mult))
                pool.tensor_tensor(se_parts[:, :, 1, :], se[:], se_hi[:].bitcast(f32), ALU.subtract)
                pool.tensor_scalar(se_parts[:, :, 0, :], se_hi[:].bitcast(f32), 1.0, 0.0, ALU.mult, ALU.add)
                done(pool.tensor_tensor(sq_a[:], sq_el[:, :, 0:1], sq_el[:, :, 1:2], ALU.add))
                done(pool.tensor_tensor(sq[:], sq_a[:], sq_el[:, :, 2:3], ALU.add))
                pool.tensor_tensor(nsq_hi[:], sq[:], minus_one1, ALU.mult)
                pt = se_parts[:].rearrange("p t a c -> p t (a c)")
                for r in range(2):
                    pool.tensor_scalar(feat[:, :, 6 * r:6 * r + 6], pt, 1.0, 0.0, ALU.mult, ALU.add)
                    pool.tensor_scalar(feat[:, :, 32 + 6 * r:35 + 6 * r], se_parts[:, :, r, :], 2.0, 0.0, ALU.mult, ALU.add)
                    last = pool.tensor_scalar(feat[:, :, 35 + 6 * r:38 + 6 * r], se_parts[:, :, 1 - r, :], 2.0, 0.0, ALU.mult, ALU.add)
                done(last)
                pool.tensor_tensor(sq_a[:], sq[:], nsq_hi[:].bitcast(f32), ALU.add)
                pool.tensor_scalar(feat[:, :, 14:15], nsq_hi[:].bitcast(f32), 1.0, 0.0, ALU.mult, ALU.add)
                done(pool.tensor_scalar(feat[:, :, 44:45], nsq_hi[:].bitcast(f32), 1.0, 0.0, ALU.mult, ALU.add))
                pool.tensor_tensor(feat[:, :, 15:16], sq_a[:], minus_one1, ALU.mult)
                pool.tensor_scalar(feat[:, :, 45:46], sq_a[:], -1.0, 0.0, ALU.mult, ALU.add).then_inc(pf, 1)

            def moments(s):
                g = [0]

                def done(ins):
                    g[0] += 1
                    ins.then_inc(pm, 1)
                    pool.wait_ge(pm, s.after(PM, g[0]))
                past(pool, xn_done, s.after(1, 0))
                pool.wait_ge(st_done, s.after(1, 1))
                pool.tensor_tensor(mo_sum[:], stats[:, :, 1:2], stats[:, :, 4:5], ALU.add)
                pool.tensor_tensor(mo_dif[:], stats[:, :, 1:2], stats[:, :, 4:5], ALU.subtract)
                done(pool.tensor_tensor(mo_dev[:], stats[:, :, 2:3], stats[:, :, 5:6], ALU.add))
                pool.tensor_tensor(mo_sq[:], mo_dif[:], mo_dif[:], ALU.mult)
                pool.tensor_scalar(mo_dev[:], mo_dev[:], 1.0 / P, EPS, ALU.mult, ALU.add)
                done(pool.tensor_scalar(mean[:], mo_sum[:], 0.5, 0.0, ALU.mult, ALU.add))
                done(pool.tensor_tensor(mo_sq[:], mo_sq[:], quarter1, ALU.mult))
                done(pool.tensor_tensor(mo_dev[:], mo_dev[:], mo_sq[:], ALU.add))
                pool.tensor_tensor(rstd[:], mo_dev[:], minus_half[:, 0:TILES].unsqueeze(2), ALU.pow).then_inc(pm, 1)

            moments(Step(0, 0))
            pool.wait_ge(s_vec, 16)
            pool.tensor_scalar(scale_c[:], vcol[:, V_V1:V_V2 + 1:4], 1.0, EPS, ALU.mult, ALU.add).then_inc(pool_pow, 1)
            pool.wait_ge(pool_pow, 1)
            pool.tensor_tensor(scale_c[:], scale_c[:], minus_half[:, 0:2], ALU.pow).then_inc(pool_pow, 1)
            pool.wait_ge(s_row, 32)
            pool.tensor_scalar(scale_r[:], vrow[:, 1, :], 1.0, EPS, ALU.mult, ALU.add).then_inc(pool_pow, 1)
            pool.wait_ge(pool_pow, 3)
            pool.tensor_tensor(scale_r[:], scale_r[:], minus_half[:], ALU.pow).then_inc(pool_pow, 1)
            factors(Step(0, 0))
            moments(Step(0, 1))

            def body(i, front, norm):
                if norm:
                    moments(i + 2)
                if front:
                    factors(i + 1)
                for k in range(2):
                    pool.wait_ge(cand_done, i.after(2, k + 1))
                    pool.tensor_tensor(dif[k][:], h[i.par()][:, halves(k)], cand[k][:], ALU.subtract).then_inc(dif_done, 1)
                    pool.wait_ge(upd_done, i.after(2, k + 1))
                    pool.wait_ge(s_res[i.par()], i.load())
                    past(pool, s_out[k], i.after(16, 0))
                    pool.tensor_tensor(y[k][:], upd[k][:], res[i.par()][:, halves(k)], ALU.add).then_inc(y_done, 1)

            steps(pool, body)

        @block.scalar
        def _(act):
            def norm_evac(s):
                for k in range(2):
                    act.wait_ge(tr_done, s.after(2, k + 1))
                    act.activation(h[s.par()][:, halves(k)], bank[B_FRONT[k]][:], ACT.Relu).then_inc(h_done, 1)
                    act.activation(h_hi[s.par()][:, halves(k)], bank[B_FRONT[k]][:], ACT.Relu).then_inc(hh_done, 1)

            def conv1_evac(s):
                for k in range(2):
                    act.wait_ge(c1_mm, s.after(2, k + 1))
                    if k == 0:
                        past(act, c1l_done, s.after(2, 0))
                    act.activation(c1[:, 2 * k:2 * k + 2, :], bank[B_FRONT[k]][:].rearrange("p (b n) -> p b n", b=2),
                                   ACT.Relu, bias=bias_c[:, 0:1], scale=scale_c[:, 0:1]).then_inc(c1_act, 1)

            def msg_evac(s):
                for q, (t0, nt) in enumerate(MSG_LOTS):
                    act.wait_ge(ms_mm, s.after(3, q + 1))
                    v = bank[B_MSG[q]][:, 0:nt * MSGW].rearrange("p (t c) -> p t c", c=MSGW)
                    if q == 0:
                        past(act, pf, s.after(PF, 0))
                    act.activation(se[:, t0:t0 + nt, :], v[:, :, P:P + 3], ACT.Copy).then_inc(se_act, 1)
                    act.activation(msg[:, t0:t0 + nt, :], v[:, :, 0:P], ACT.Relu).then_inc(ms_act, 1)

            def factor_evac(s):
                for k in range(2):
                    act.wait_ge(ft_mm, s.after(2, k + 1))
                    act.activation(f_nb[0:16, halves(k)], bank[B_FRONT[k]][0:16, :], ACT.Copy)
                    act.activation(f_nd[0:16, halves(k)], bank[B_FRONT[k]][32:48, :], ACT.Copy).then_inc(ft_act, 1)

            def exps(s):
                for b in range(STEP_B):
                    act.wait_ge(di_mm, s.after(STEP_B, b + 1))
                    act.activation(aff[:, b, :], bank[B_DIST[b]][:], ACT.Exp).then_inc(exp_done, 1)

            def agg_evac(s):
                for k in range(2):
                    act.wait_ge(ag_mm, s.after(2, k + 1))
                    act.activation(agg_hi[:, halves(k)], bank[B_AGG[k]][:], ACT.Copy).then_inc(agh_done, 1)

            def conv2_evac(i, k):
                act.wait_ge(c2_mm, i.after(2, k + 1))
                past(act, xcl_done, i.after(2, 0))
                act.activation(xc[:, halves(k)], bank[B_C2[k]][:], ACT.Relu, bias=bias_c[:, 1:2]).then_inc(xc_done, 1)

            def gate_tanh(i, k):
                act.wait_ge(g_mm, i.after(8, 4 * k + 1))
                act.activation(tr[k][:], bank[B_R][:], ACT.Tanh, bias=bias_c[:, 2:3], scale=0.5).then_inc(tr_act, 1)
                act.wait_ge(g_mm, i.after(8, 4 * k + 2))
                act.activation(tz[k][:], bank[B_Z][:], ACT.Tanh, bias=bias_c[:, 3:4], scale=0.5).then_inc(tz_act, 1)

            def cand_tanh(i, k):
                act.wait_ge(pre_done, i.after(2, k + 1))
                past(act, upd_done, i.after(2, 0))
                act.activation(cand[k][:], pre[k][:], ACT.Tanh, bias=bias_c[:, 4:5]).then_inc(cand_done, 1)

            act.wait_ge(dve_set, 5)
            z = Step(0, 0)
            norm_evac(z)
            conv1_evac(z)
            msg_evac(z)
            act.wait_ge(w_ready, 4)
            factor_evac(z)
            exps(z)
            agg_evac(z)

            def body(i, front, norm):
                if front:
                    past(act, dif_done, i.after(2, 0))
                    norm_evac(i + 1)
                conv2_evac(i, 0)
                if front:
                    conv1_evac(i + 1)
                    msg_evac(i + 1)
                    factor_evac(i + 1)
                conv2_evac(i, 1)
                gate_tanh(i, 0)
                if front:
                    exps(i + 1)
                cand_tanh(i, 0)
                gate_tanh(i, 1)
                cand_tanh(i, 1)
                if front:
                    agg_evac(i + 1)

            steps(act, body)

        @block.vector
        def _(dve):
            chain = [0]

            def link(ins):
                chain[0] += 1
                ins.then_inc(dve_set, 1)
                dve.wait_ge(dve_set, chain[0])

            def norm_stats(s):
                dve.wait_ge(s_x[s.par()], s.load())
                past(dve, pm, s.after(PM, 0))
                for t in range(TILES):
                    last = dve.bn_stats(stats[:, t, :], xt[s.par()][:, t, :])
                last.then_inc(st_done, 1)
            def norm_apply(s):
                dve.wait_ge(pm, s.after(PM, PM))
                past(dve, tr_done, s.after(2, 0))
                for t in range(TILES):
                    last = dve.tensor_scalar(xn[:, t, :], xt[s.par()][:, t, :], mean[:, t, :], rstd[:, t, :],
                                             ALU.subtract, ALU.mult)
                last.then_inc(xn_done, 1)

            def norm_split(s):
                for k in range(2):
                    dve.wait_ge(hh_done, s.after(2, k + 1))
                    dve.tensor_tensor(h_lo[s.par()][:, halves(k)], h[s.par()][:, halves(k)],
                                      h_hi[s.par()][:, halves(k)].bitcast(f32), ALU.subtract).then_inc(hl_done, 1)

            def conv1_split(s):
                for k in range(2):
                    b = slice(2 * k, 2 * k + 2)
                    dve.wait_ge(c1_act, s.after(2, k + 1))
                    hi = c1_hi[s.par()][:, b, PAD:PAD + N_NODE]
                    dve.tensor_copy(hi, c1[:, b, :]).then_inc(c1h_done, 1)
                    dve.wait_ge(c1h_done, s.after(2, k + 1))
                    dve.tensor_tensor(c1_lo[s.par()][:, b, PAD:PAD + N_NODE], c1[:, b, :], hi.bitcast(f32),
                                      ALU.subtract).then_inc(c1l_done, 1)

            def masks(s):
                dve.wait_ge(s_mask[s.par()], s.load())
                for b in range(STEP_B):
                    dve.wait_ge(exp_done, s.after(STEP_B, b + 1))
                    dve.tensor_tensor(aff[:, b, :], aff[:, b, :], mask[s.par()][:, b, :], ALU.mult).then_inc(aff_done, 1)

            def agg_split(s):
                for k in range(2):
                    dve.wait_ge(agh_done, s.after(2, k + 1))
                    dve.tensor_tensor(agg_lo[:, halves(k)], bank[B_AGG[k]][:], agg_hi[:, halves(k)].bitcast(f32),
                                      ALU.subtract).then_inc(agl_done, 1)

            def conv2_split(i, k):
                dve.wait_ge(xc_done, i.after(2, k + 1))
                dve.tensor_copy(xc_hi[:, halves(k)], xc[:, halves(k)]).then_inc(xch_done, 1)
                dve.wait_ge(xch_done, i.after(2, k + 1))
                dve.tensor_tensor(xc_lo[:, halves(k)], xc[:, halves(k)], xc_hi[:, halves(k)].bitcast(f32),
                                  ALU.subtract).then_inc(xcl_done, 1)

            def candidate(i, k):
                dve.wait_ge(tr_act, i.after(2, k + 1))
                dve.wait_ge(g_mm, i.after(8, 4 * k + 3))
                dve.scalar_tensor_tensor(rg[k][:], tr[k][:], 1.0, bank[B_GN][:], ALU.add, ALU.mult).then_inc(rg_done, 1)
                dve.wait_ge(rg_done, i.after(2, k + 1))
                dve.wait_ge(g_mm, i.after(8, 4 * k + 4))
                dve.tensor_tensor(pre[k][:], rg[k][:], bank[B_IN][:], ALU.add).then_inc(pre_done, 1)

            def update(i, k):
                dve.wait_ge(dif_done, i.after(2, k + 1))
                dve.wait_ge(tz_act, i.after(2, k + 1))
                dve.scalar_tensor_tensor(zd[k][:], tz[k][:], 1.0, dif[k][:], ALU.add, ALU.mult).then_inc(zd_done, 1)
                dve.wait_ge(zd_done, i.after(2, k + 1))
                past(dve, y_done, i.after(2, 0))
                dve.scalar_tensor_tensor(upd[k][:], zd[k][:], 0.5, cand[k][:], ALU.mult, ALU.add).then_inc(upd_done, 1)

            z = Step(0, 0)
            norm_stats(z)
            norm_apply(z)
            dve.wait_ge(s_vec, 16)
            dve.wait_ge(pool_pow, 2)
            link(dve.tensor_tensor(scale_c[:], scale_c[:], vcol[:, V_G1:V_G2 + 1:4], ALU.mult))
            link(dve.tensor_tensor(tmp_c[:], scale_c[:], vcol[:, V_M1:V_M2 + 1:4], ALU.mult))
            link(dve.tensor_tensor(bias_c[:, 0:2], vcol[:, V_B1:V_B2 + 1:4], tmp_c[:], ALU.subtract))
            link(dve.tensor_tensor(bias_c[:, 2:4], vcol[:, V_IR:V_IZ + 1], vcol[:, V_HR:V_HZ + 1], ALU.add))
            dve.tensor_copy(bias_c[:, 4:5], vcol[:, V_IN:V_IN + 1])
            link(dve.tensor_scalar(bias_c[:, 2:4], bias_c[:, 2:4], 0.5, None, ALU.mult))
            dve.wait_ge(s_w1, 16)
            link(dve.tensor_copy(w1_hi[:], w1_raw[:]))
            dve.tensor_tensor(w1_lo[:], w1_raw[:], w1_hi[:].bitcast(f32), ALU.subtract).then_inc(w_ready, 1)
            norm_split(z)
            dve.wait_ge(s_row, 32)
            dve.wait_ge(pool_set, 10)
            dve.tensor_copy(ones[:], ones32[:])
            dve.tensor_copy(bias_msg[:], zeros32[:, 0:3 * MSGW])
            dve.tensor_copy(f_nb[:], zeros32[:])
            dve.tensor_copy(f_nd[:], zeros32[:])
            link(dve.tensor_copy(mrow_hi[:], mrow[:]))
            dve.tensor_copy(bias_msg[0:1, :], mrow_hi[0:1, :].bitcast(f32))
            dve.tensor_tensor(bias_msg[32:33, :], mrow[32:33, :], mrow_hi[32:33, :].bitcast(f32), ALU.subtract).then_inc(w_ready, 1)
            conv1_split(z)
            for k in range(2):
                for c in (c1_hi, c1_lo):
                    for edge in (0, PAD + N_NODE):
                        last = dve.tensor_copy(c[k][:, :, edge:edge + PAD], zeros32[:, 0:STEP_B * PAD].rearrange("p (b e) -> p b e", b=STEP_B))
            last.then_inc(w_ready, 2)
            masks(z)
            norm_stats(z + 1)
            norm_apply(z + 1)
            dve.wait_ge(s_wg, 16)
            link(dve.tensor_scalar(wg_raw[:, 0, 2 * P:3 * P], wg_raw[:, 0, 2 * P:3 * P], 0.5, None, ALU.mult))
            link(dve.tensor_copy(wg_hi[:], wg_raw[:]))
            dve.tensor_tensor(wg_lo[:], wg_raw[:], wg_hi[:].bitcast(f32), ALU.subtract)
            dve.tensor_copy(bias_ghn[:], zeros32[:, 0:P])
            dve.tensor_copy(ident_r[:], ident[:])
            link(dve.tensor_scalar(ghn_row[:], vrow[:, 2, :], 0.5, None, ALU.mult))
            link(dve.tensor_copy(ghn_hi[:], ghn_row[:]))
            dve.tensor_copy(bias_ghn[0:1, :], ghn_hi[0:1, :].bitcast(f32))
            dve.tensor_tensor(bias_ghn[32:33, :], ghn_row[32:33, :], ghn_hi[32:33, :].bitcast(f32), ALU.subtract).then_inc(w_ready, 1)
            dve.wait_ge(pool_pow, 4)
            link(dve.tensor_tensor(scale_r[:], scale_r[:], vrow[:, 0, :], ALU.mult))
            dve.wait_ge(s_w2, 16)
            link(dve.tensor_tensor(w2_raw[:], w2_raw[:], scale_r[:].unsqueeze(1).to_broadcast([P, TAPS, P]), ALU.mult))
            link(dve.tensor_copy(w2_hi[:], w2_raw[:]))
            dve.tensor_tensor(w2_lo[:], w2_raw[:], w2_hi[:].bitcast(f32), ALU.subtract).then_inc(w_ready, 1)
            agg_split(z)

            def body(i, front, norm_on):
                if front:
                    norm_split(i + 1)
                if norm_on:
                    norm_stats(i + 2)
                conv2_split(i, 0)
                if front:
                    conv1_split(i + 1)
                if norm_on:
                    norm_apply(i + 2)
                conv2_split(i, 1)
                candidate(i, 0)
                if front:
                    masks(i + 1)
                update(i, 0)
                candidate(i, 1)
                update(i, 1)
                if front:
                    agg_split(i + 1)

            steps(dve, body)

        @block.tensor
        def _(pe):
            def mm(out_, w, x, start, stop):
                return pe.matmul(out_, w, x, start=start, stop=stop)

            def products(terms):
                return [(w, x) for (wh, wl), (xh, xl) in terms for w, x in ((wh, xh), (wh, xl), (wl, xh))]

            def group(out_, terms, extra=()):
                pairs = list(extra) + products(terms)
                for q, (w, x) in enumerate(pairs):
                    last = mm(out_, w, x, q == 0, q == len(pairs) - 1)
                return last

            def transpose_x(s):
                pe.wait_ge(xn_done, s.after(1, 1))
                for k in range(2):
                    for t in range(TILES // 2):
                        last = pe.transpose(bank[B_FRONT[k]][:, t * P:(t + 1) * P], xn[:, k * TILES // 2 + t, :], ident[:])
                    last.then_inc(tr_done, 1)

            def conv1(s):
                p = s.par()
                pe.wait_ge(hl_done, s.after(2, 2))
                for k in range(2):
                    group(bank[B_FRONT[k]][:], [((w1_hi[:], w1_lo[:]), (h_hi[p][:, halves(k)], h_lo[p][:, halves(k)]))])\
                        .then_inc(c1_mm, 1)

            def messages(s):
                for q, (t0, nt) in enumerate(MSG_LOTS):
                    mm(bank[B_MSG[q]][:, 0:nt * MSGW], ones[:, 0:P], bias_msg[:, 0:nt * MSGW], True, False)
                    for t in range(nt):
                        last = mm(bank[B_MSG[q]][:, t * MSGW:(t + 1) * MSGW], h[s.par()][:, (t0 + t) * P:(t0 + t + 1) * P],
                                  wm_sb[:], False, t == nt - 1)
                    last.then_inc(ms_mm, 1)

            def transpose_factors(s):
                pe.wait_ge(pf, s.after(PF, PF))
                pe.wait_ge(c1_act, s.after(2, 2))
                for k in range(2):
                    for t in range(TILES // 2):
                        last = pe.transpose(bank[B_FRONT[k]][:, t * P:(t + 1) * P], feat[:, k * TILES // 2 + t, :], ident[:])
                    last.then_inc(ft_mm, 1)

            def distances(s):
                for b in range(STEP_B):
                    pe.wait_ge(ft_act, s.after(2, b // 2 + 1 if b else 2))
                    for m in range(MT):
                        at = b * N_NODE
                        last = mm(bank[B_DIST[b]][:, m * N_NODE:(m + 1) * N_NODE], f_nb[:, at + m * P:at + (m + 1) * P],
                                  f_nd[:, at:at + N_NODE], True, True)
                    last.then_inc(di_mm, 1)

            def aggregate(s):
                pe.wait_ge(exp_done, s.after(STEP_B, STEP_B))
                for b in range(STEP_B):
                    pe.wait_ge(aff_done, s.after(STEP_B, b + 1))
                    for m in range(MT):
                        last = mm(bank[B_AGG[b // 2]][:, (b % 2) * N_NODE:(b % 2 + 1) * N_NODE], msg[:, b * MT + m, :],
                                  aff[:, b, m * N_NODE:(m + 1) * N_NODE], m == 0, m == MT - 1)
                    if b % 2:
                        last.then_inc(ag_mm, 1)

            def conv2(i, k):
                p = i.par()
                c = slice(2 * k, 2 * k + 2)
                o = bank[B_C2[k]][:].rearrange("p (b n) -> p b n", b=2)
                keep = [(ident_r[:], x[p][:, halves(k)].rearrange("p (b n) -> p b n", b=2)) for x in (h_hi, h_lo)]
                group(o, [((w2_hi[:, t, :], w2_lo[:, t, :]), (c1_hi[p][:, c, t:t + N_NODE], c1_lo[p][:, c, t:t + N_NODE]))
                          for t in range(TAPS)], keep).then_inc(c2_mm, 1)

            def gates(i, k):
                p = i.par()
                hid = (h_hi[p][:, halves(k)], h_lo[p][:, halves(k)])
                con = (xc_hi[:, halves(k)], xc_lo[:, halves(k)])
                agg = (agg_hi[:, halves(k)], agg_lo[:, halves(k)])

                def w(src, gate):
                    return wg_hi[:, src, gate * P:(gate + 1) * P], wg_lo[:, src, gate * P:(gate + 1) * P]
                group(bank[B_R][:], [(w(0, 0), hid), (w(2, 0), agg), (w(1, 0), con)]).then_inc(g_mm, 1)
                if k:
                    pe.wait_ge(tz_act, i.after(2, k))
                group(bank[B_Z][:], [(w(0, 1), hid), (w(2, 1), agg), (w(1, 1), con)]).then_inc(g_mm, 1)
                if k:
                    pe.wait_ge(rg_done, i.after(2, k))
                group(bank[B_GN][:], [(w(0, 2), hid)], [(bias_ghn[:], ones[:])]).then_inc(g_mm, 1)
                if k:
                    pe.wait_ge(pre_done, i.after(2, k))
                else:
                    past(pe, pre_done, i.after(2, 0))
                group(bank[B_IN][:], [(w(2, 2), agg), (w(1, 2), con)]).then_inc(g_mm, 1)

            z = Step(0, 0)
            pe.wait_ge(pool_set, 10)
            transpose_x(z)
            pe.wait_ge(w_ready, 1)
            conv1(z)
            pe.wait_ge(s_wm, 16)
            pe.wait_ge(w_ready, 2)
            messages(z)
            transpose_factors(z)
            distances(z)
            aggregate(z)
            pe.wait_ge(w_ready, 6)

            def body(i, front, norm):
                if front:
                    transpose_x(i + 1)
                pe.wait_ge(c1l_done, i.after(2, 2))
                pe.wait_ge(exp_done, i.after(STEP_B, STEP_B))
                conv2(i, 0)
                if front:
                    conv1(i + 1)
                    past(pe, pre_done, i.after(2, 0))
                    pe.wait_ge(agl_done, i.after(2, 2))
                    messages(i + 1)
                else:
                    pe.wait_ge(agl_done, i.after(2, 2))
                conv2(i, 1)
                if front:
                    transpose_factors(i + 1)
                    pe.wait_ge(ms_act, (i + 1).after(3, 3))
                pe.wait_ge(xcl_done, i.after(2, 1))
                gates(i, 0)
                pe.wait_ge(xcl_done, i.after(2, 2))
                if front:
                    distances(i + 1)
                pe.wait_ge(tr_act, i.after(2, 1))
                gates(i, 1)
                if front:
                    pe.wait_ge(tr_act, i.after(2, 2))
                    aggregate(i + 1)

            steps(pe, body)


_VECTORS = ["bn1_g", "bn1_b", "bn1_m", "bn1_v", "bn2_g", "bn2_b", "bn2_m", "bn2_v"]


def kernel(**inputs):
    import numpy as np
    import concourse.bacc as bacc
    from concourse import mybir
    from concourse.bass_utils import run_bass_kernel_spmd

    a = {k.replace("L0_gnn_", ""): np.asarray(v) for k, v in inputs.items()}
    x, adj = a["x"], a["adj"]
    vectors = np.concatenate([np.stack([a[n] for n in _VECTORS]), a["b_ih"].reshape(3, P), a["b_hh"].reshape(3, P)])
    w_ih, w_hh = a["w_ih"], a["w_hh"]
    arrays = {
        "x_tok": x.reshape(STEPS, TILES, P, P).transpose(0, 2, 1, 3),
        "x_chan": x.reshape(STEPS, STEP_TOK, P).transpose(0, 2, 1),
        "mask_t": adj.transpose(0, 2, 1).reshape(STEPS, STEP_B, MT, P, N_NODE).transpose(0, 3, 1, 2, 4).reshape(STEPS, P, STEP_B, HALF),
        "vec_col": vectors.T,
        "vec_row": np.concatenate([a["bn2_g"], a["bn2_v"], a["b_hh"][2 * P:]]).reshape(1, 3 * P),
        "msg_row": np.tile(np.concatenate([a["b_msg"], a["b_se"], np.zeros(1, np.float32)]), 3).reshape(1, 3 * MSGW),
        "w1": a["conv1_w"][:, :, 0].T,
        "w2": a["conv2_w"].transpose(1, 2, 0),
        "wg": np.stack([w_hh.T, w_ih[:, :P].T, w_ih[:, P:].T], axis=1),
        "wm": np.concatenate([a["w_msg"].T, a["w_se"].T, np.zeros((P, 1), np.float32)], axis=1),
    }
    arrays = {k: np.ascontiguousarray(v) for k, v in arrays.items()}
    nc = bacc.Bacc("TRN2", target_bir_lowering=False, num_devices=1)
    args = [nc.dram_tensor(n, v.shape, mybir.dt.from_np(v.dtype), kind="ExternalInput").ap() for n, v in arrays.items()]
    out = nc.dram_tensor("out", (STEPS, P, STEP_TOK), mybir.dt.float32, kind="ExternalOutput").ap()
    gnn_layer(nc, *args, out)
    r = run_bass_kernel_spmd(nc, [arrays], core_ids=[0])
    return r.results[0]["out"].transpose(0, 2, 1).reshape(N_BATCH, N_NODE, P)
```

```python
import concourse.bass as bass
from concourse import mybir
from contextlib import ExitStack

P = 128
N_BATCH, N_NODE = 32, 256
STEP_B = 4
STEP_TOK = STEP_B * N_NODE
STEPS = N_BATCH // STEP_B
TILES = STEP_TOK // P
HALF = 512
MT = N_NODE // P
TAPS, PAD = 17, 8
ROW = N_NODE + 2 * PAD + 4
QN = N_NODE // 4
QB = STEP_B * QN
QROW = QN + 4
SROW = 2 * QROW + 2
NW2 = TAPS + 20
MSGW = P + 4
EPS = 1e-5
(V_G1, V_B1, V_M1, V_V1, V_G2, V_B2, V_M2, V_V2, V_IR, V_IZ, V_IN, V_HR, V_HZ, V_HN) = range(14)
NVEC = 14


def gnn_layer(nc, x_tok, x_chan, mask_t, vec_col, msg_row, w1, w2, wg, wm, out):
    f32, f32r = mybir.dt.float32, mybir.dt.float32r
    ALU, ACT, AX = mybir.AluOpType, mybir.ActivationFunctionType, mybir.AxisListType
    ctx = ExitStack()
    with ctx:
        def sb(name, shape, dt=f32):
            return ctx.enter_context(nc.sbuf_tensor(name, shape, dt))

        def sem(name):
            return ctx.enter_context(nc.semaphore(name))

        vcol = sb("vcol", [P, NVEC])
        mrow = sb("mrow", [P, MSGW])
        w1_raw = sb("w1_raw", [P, P])
        back = sb("back", [P, 12 * HALF])
        w2_raw = back[:, 0:NW2 * P].rearrange("p (t c) -> p t c", c=P)
        wg_raw = back[:, NW2 * P:(NW2 + 9) * P].rearrange("p (s c) -> p s c", s=3)
        wm_sb = sb("wm_sb", [P, MSGW])
        w1_hi, w1_lo = sb("w1_hi", [P, P], f32r), sb("w1_lo", [P, P], f32r)
        w2_hi, w2_lo = sb("w2_hi", [P, NW2, P], f32r), sb("w2_lo", [P, NW2, P], f32r)
        wg_hi, wg_lo = sb("wg_hi", [P, 3, 3 * P], f32r), sb("wg_lo", [P, 3, 3 * P], f32r)
        ident = sb("ident", [P, P])
        ones = sb("ones", [P, HALF], f32r)
        ones32 = sb("ones32", [P, 3 * TILES])
        scale_w = sb("scale_w", [P, P])
        scale_c = sb("scale_c", [P, 2])
        bias_c = sb("bias_c", [P, 6])
        tmp_c = sb("tmp_c", [P, 2])
        minus_half = sb("minus_half", [P, TILES])
        minus_one, quarter = sb("minus_one", [P, TILES]), sb("quarter", [P, TILES])
        mrow_hi = sb("mrow_hi", [P, MSGW], f32r)
        bias_msg = sb("bias_msg", [P, 3 * MSGW], f32r)
        xt = [sb(f"xt{k}", [P, TILES, P]) for k in range(2)]
        stats = sb("stats", [P, TILES, 6])
        mo_sum, mo_dif, mo_dev, mo_sq, mean, rstd = (sb(n, [P, TILES, 1]) for n in ("mo_sum", "mo_dif", "mo_dev", "mo_sq", "mean", "rstd"))
        h = [sb(f"h{k}", [P, STEP_TOK]) for k in range(2)]
        h_hi = [sb(f"h_hi{k}", [P, STEP_TOK], f32r) for k in range(2)]
        h_lo = [sb(f"h_lo{k}", [P, STEP_TOK], f32r) for k in range(2)]
        c1 = sb("c1", [P, STEP_B, ROW])
        half_dif = sb("half_dif", [P, 2, STEP_B, SROW])
        quart_dif = sb("quart_dif", [P, 3, 2, STEP_B, QROW])
        quart_hi = sb("quart_hi", [P, 3, 3, STEP_B, QROW], f32r)
        quart_lo = sb("quart_lo", [P, 3, 3, STEP_B, QROW], f32r)
        msg = sb("msg", [P, TILES, P])
        se = sb("se", [P, TILES, 3])
        se_hi = sb("se_hi", [P, TILES, 3], f32r)
        sq_el = sb("sq_el", [P, TILES, 3])
        sq, sq_a = sb("sq", [P, TILES, 1]), sb("sq_a", [P, TILES, 1])
        nsq_hi = sb("nsq_hi", [P, TILES, 1], f32r)
        se_parts = sb("se_parts", [P, TILES, 2, 3])
        feat = sb("feat", [P, TILES, 2, 32])
        feat_t = sb("feat_t", [P, TILES, 2, 32])
        factor = sb("factor", [P, 2, STEP_TOK], f32r)
        mask = sb("mask", [P, STEP_B, HALF])
        aff = sb("aff", [P, STEP_B, HALF])
        agg_hi, agg_lo = sb("agg_hi", [P, STEP_TOK], f32r), sb("agg_lo", [P, STEP_TOK], f32r)
        xc = back[:, 0:STEP_TOK]
        tr, tz, cand, dif = ([back[:, (2 + 2 * q + k) * HALF:(3 + 2 * q + k) * HALF] for k in range(2)] for q in range(4))
        ghn = cand
        rg = pre = tr
        zd = upd = dif
        p_sum = back[:, 10 * HALF:11 * HALF]
        pp = sb("pp", [P, HALF // 2])
        xc_hi, xc_lo = sb("xc_hi", [P, STEP_TOK], f32r), sb("xc_lo", [P, STEP_TOK], f32r)
        res = [sb(f"res{k}", [P, STEP_TOK]) for k in range(2)]
        bank = [ctx.enter_context(nc.psum_tensor(f"bank{k}", [P, HALF], f32)) for k in range(8)]
        B_PR = (0, 3, 0)
        B_PP = 1
        B_FRONT = (2, 3)
        B_MSG = (4, 5, 6)
        B_R, B_Z, B_GN, B_IN = 4, 5, 6, 7
        B_DIST = (2, 3, 0, 1)
        B_AGG = (4, 5)
        MSG_LOTS = [(0, 3), (3, 3), (6, 2)]

        s_vec, s_row, s_w1, s_w2, s_wg, s_wm = (sem(n) for n in ("s_vec", "s_row", "s_w1", "s_w2", "s_wg", "s_wm"))
        s_x = [sem(f"s_x{k}") for k in range(2)]
        s_res = [sem(f"s_res{k}") for k in range(2)]
        s_mask = sem("s_mask")
        s_out = [sem(f"s_out{k}") for k in range(2)]
        pool_set = sem("pool_set")
        act_set = sem("act_set")
        dve_fill, w2_scale, w2_done = sem("dve_fill"), sem("w2_scale"), sem("w2_done")
        sum_lo = sem("sum_lo")
        pool_pow = sem("pool_pow")
        dve_set = sem("dve_set")
        w_ready = sem("w_ready")
        st_done, pm, xn_done = sem("st_done"), sem("pm"), sem("xn_done")
        tr_done = sem("tr_done")
        h_done, hh_done, hl_done = sem("h_done"), sem("hh_done"), sem("hl_done")
        c1_mm, c1_act = sem("c1_mm"), sem("c1_act")
        hd_done, qd_done, qh_done, ql_done = sem("hd_done"), sem("qd_done"), sem("qh_done"), sem("ql_done")
        ms_mm, ms_act, se_act = sem("ms_mm"), sem("ms_act"), sem("se_act")
        pf = sem("pf")
        ft_done, fc_dve, fc_act = sem("ft_done"), sem("fc_dve"), sem("fc_act")
        di_mm, exp_done, aff_done = sem("di_mm"), sem("exp_done"), sem("aff_done")
        ag_mm, agh_done, agl_done = sem("ag_mm"), sem("agh_done"), sem("agl_done")
        c2_mm = sem("c2_mm")
        pp_act, ps_done, qs_done, yc_done = sem("pp_act"), sem("ps_done"), sem("qs_done"), sem("yc_done")
        xs_done, xc_done, xch_done, xcl_done = sem("xs_done"), sem("xc_done"), sem("xch_done"), sem("xcl_done")
        g_mm = sem("g_mm")
        gn_mm, gn_act = sem("gn_mm"), sem("gn_act")
        tr_act, tz_act, rg_done, pre_done, cand_done = (sem(n) for n in ("tr_act", "tz_act", "rg_done", "pre_done", "cand_done"))
        dif_done, zd_done, upd_done, y_done = sem("dif_done"), sem("zd_done"), sem("upd_done"), sem("y_done")
        PF, PM = 6, 5

        class Step:
            def __init__(self, j, c):
                self.j, self.c = j, c

            def __add__(self, d):
                return Step(self.j, self.c + d)

            def par(self):
                return self.c % 2

            def n(self):
                return self.j * 2 + self.c

            def after(self, per, k):
                return self.j * (2 * per) + (self.c * per + k)

            def load(self):
                return self.j * 16 + 16 * (self.c // 2 + 1)

        def steps(eng, body):
            body(Step(0, 0), True, True)
            body(Step(0, 1), True, True)
            with eng.Fori(1, (STEPS - 2) // 2) as j:
                body(Step(j, 0), True, True)
                body(Step(j, 1), True, True)
            body(Step((STEPS - 2) // 2, 0), True, False)
            body(Step((STEPS - 2) // 2, 1), False, False)

        def past(eng, semaphore, value):
            if not isinstance(value, int) or value > 0:
                eng.wait_ge(semaphore, value)

        def halves(k):
            return slice(k * HALF, (k + 1) * HALF)

        def half_seq(c):
            return (c1[:], 1, 2) if c == 0 else (half_dif[:, c - 1], 0, 1)

        def evens(x, first, step, n):
            return bass.AP(x.tensor, x.offset + first, [x.ap[0], [2 * step, 2], x.ap[-2], [2 * step, n]])

        def odds(x, first, step, n):
            return bass.AP(x.tensor, x.offset + first + step, [x.ap[0], x.ap[-2], [2 * step, n]])

        def twice(x):
            return x.unsqueeze(1).to_broadcast([P, 2] + list(x.shape[1:]))

        def flat(x):
            return x.rearrange("p a b v -> p (a b v)")

        def factor_rows(q):
            return factor[0:16].rearrange("f s (t q j) -> f t s q j", q=4, j=32)[:, :, :, q, :]

        def phases(x, c):
            return x.rearrange("p (t f) -> p f t", f=4)[:, c - 1:4:2]

        def two(x):
            return x.rearrange("p (f n) -> p f n", f=2)

        block = ctx.enter_context(nc.Block())

        @block.sync
        def _(sp):
            def load_x(s):
                sp.dma_start(xt[s.par()][:], x_tok[bass.ds(s.n(), 1)].rearrange("o p t c -> p (o t) c")).then_inc(s_x[s.par()], 16)

            def load_mask(s):
                sp.dma_start(mask[:], mask_t[bass.ds(s.n(), 1)].rearrange("o p b n -> p (o b) n")).then_inc(s_mask, 16)

            def load_res(s):
                sp.dma_start(res[s.par()][:], x_chan[bass.ds(s.n(), 1)].rearrange("o p t -> p (o t)")).then_inc(s_res[s.par()], 16)

            first = Step(0, 0)
            load_x(first)
            sp.dma_start(w1_raw[:], w1).then_inc(s_w1, 16)
            sp.dma_start(vcol[:], vec_col).then_inc(s_vec, 16)
            sp.dma_start(mrow[:], msg_row.to_broadcast([P, MSGW])).then_inc(s_row, 16)
            sp.dma_start(wm_sb[:], wm).then_inc(s_wm, 16)
            sp.dma_start(w2_raw[:, 0:TAPS], w2).then_inc(s_w2, 16)
            load_x(first + 1)
            sp.dma_start(wg_raw, wg).then_inc(s_wg, 16)
            load_mask(first)
            load_res(first)

            def body(i, front, norm):
                if norm:
                    sp.wait_ge(tr_done, i.after(2, 2))
                    load_x(i + 2)
                if front:
                    sp.wait_ge(aff_done, i.after(STEP_B, STEP_B))
                    load_mask(i + 1)
                    for k in range(2):
                        past(sp, s_out[k], i.after(16, 0))
                    load_res(i + 1)
                for k in range(2):
                    sp.wait_ge(y_done, i.after(2, k + 1))
                    sp.dma_start(out[bass.ds(i.n(), 1), :, halves(k)].rearrange("o p t -> p (o t)"), res[i.par()][:, halves(k)]).then_inc(s_out[k], 16)

            steps(sp, body)
            for k in range(2):
                sp.wait_ge(s_out[k], 16 * STEPS)

        @block.gpsimd
        def _(pool):
            chain = [0]

            def link(ins):
                chain[0] += 1
                ins.then_inc(pool_set, 1)
                pool.wait_ge(pool_set, chain[0])

            pool.memset(minus_half[:], -0.5)
            pool.memset(quarter[:], 0.25)
            pool.memset(minus_one[:], -1.0)
            pool.memset(ones32[:], 1.0)
            pool.memset(feat[:], 0.0)
            link(pool.memset(ident[:], 0.0))
            link(pool.affine_select(out=ident[:], in_=ident[:], compare_op=ALU.not_equal, fill=1.0, base=0,
                                    pattern=[[-1, P]], channel_multiplier=1))
            pool.memset(feat[:, :, 0, 12:14], 1.0)
            link(pool.memset(feat[:, :, 1, 14:16], 1.0))
            one3 = ones32[:, 0:3 * TILES].rearrange("p (t c) -> p t c", c=3)
            minus_one1, quarter1 = minus_one[:].unsqueeze(2), quarter[:].unsqueeze(2)

            def factors(s):
                g = [0]

                def done(ins):
                    g[0] += 1
                    ins.then_inc(pf, 1)
                    pool.wait_ge(pf, s.after(PF, g[0]))
                past(pool, ft_done, s.after(1, 0))
                pool.wait_ge(se_act, s.after(3, 3))
                pool.tensor_tensor(se_hi[:], se[:], one3, ALU.mult)
                done(pool.tensor_tensor(sq_el[:], se[:], se[:], ALU.mult))
                pool.tensor_tensor(se_parts[:, :, 1, :], se[:], se_hi[:].bitcast(f32), ALU.subtract)
                pool.tensor_scalar(se_parts[:, :, 0, :], se_hi[:].bitcast(f32), 1.0, 0.0, ALU.mult, ALU.add)
                done(pool.tensor_tensor(sq_a[:], sq_el[:, :, 0:1], sq_el[:, :, 1:2], ALU.add))
                done(pool.tensor_tensor(sq[:], sq_a[:], sq_el[:, :, 2:3], ALU.add))
                pool.tensor_tensor(nsq_hi[:], sq[:], minus_one1, ALU.mult)
                pt = se_parts[:].rearrange("p t a c -> p t (a c)")
                for r in range(2):
                    pool.tensor_scalar(feat[:, :, 0, 6 * r:6 * r + 6], pt, 1.0, 0.0, ALU.mult, ALU.add)
                    pool.tensor_scalar(feat[:, :, 1, 6 * r:3 + 6 * r], se_parts[:, :, r, :], 2.0, 0.0, ALU.mult, ALU.add)
                    last = pool.tensor_scalar(feat[:, :, 1, 3 + 6 * r:6 + 6 * r], se_parts[:, :, 1 - r, :], 2.0, 0.0, ALU.mult, ALU.add)
                done(last)
                pool.tensor_tensor(sq_a[:], sq[:], nsq_hi[:].bitcast(f32), ALU.add)
                pool.tensor_scalar(feat[:, :, 0, 14:15], nsq_hi[:].bitcast(f32), 1.0, 0.0, ALU.mult, ALU.add)
                done(pool.tensor_scalar(feat[:, :, 1, 12:13], nsq_hi[:].bitcast(f32), 1.0, 0.0, ALU.mult, ALU.add))
                pool.tensor_tensor(feat[:, :, 0, 15:16], sq_a[:], minus_one1, ALU.mult)
                pool.tensor_scalar(feat[:, :, 1, 13:14], sq_a[:], -1.0, 0.0, ALU.mult, ALU.add).then_inc(pf, 1)

            def moments(s):
                g = [0]

                def done(ins):
                    g[0] += 1
                    ins.then_inc(pm, 1)
                    pool.wait_ge(pm, s.after(PM, g[0]))
                past(pool, xn_done, s.after(2, 0))
                pool.wait_ge(st_done, s.after(1, 1))
                pool.tensor_tensor(mo_sum[:], stats[:, :, 1:2], stats[:, :, 4:5], ALU.add)
                pool.tensor_tensor(mo_dif[:], stats[:, :, 1:2], stats[:, :, 4:5], ALU.subtract)
                done(pool.tensor_tensor(mo_dev[:], stats[:, :, 2:3], stats[:, :, 5:6], ALU.add))
                pool.tensor_tensor(mo_sq[:], mo_dif[:], mo_dif[:], ALU.mult)
                pool.tensor_scalar(mo_dev[:], mo_dev[:], 1.0 / P, EPS, ALU.mult, ALU.add)
                done(pool.tensor_scalar(mean[:], mo_sum[:], 0.5, 0.0, ALU.mult, ALU.add))
                done(pool.tensor_tensor(mo_sq[:], mo_sq[:], quarter1, ALU.mult))
                done(pool.tensor_tensor(mo_dev[:], mo_dev[:], mo_sq[:], ALU.add))
                pool.tensor_tensor(rstd[:], mo_dev[:], minus_half[:].unsqueeze(2), ALU.pow).then_inc(pm, 1)

            moments(Step(0, 0))
            pool.wait_ge(s_vec, 16)
            pool.tensor_scalar(scale_c[:], vcol[:, V_V1:V_V2 + 1:4], 1.0, EPS, ALU.mult, ALU.add).then_inc(pool_pow, 1)
            pool.wait_ge(pool_pow, 1)
            pool.tensor_tensor(scale_c[:], scale_c[:], minus_half[:, 0:2], ALU.pow).then_inc(pool_pow, 1)
            pool.memset(factor[:].bitcast(f32), 0.0).then_inc(pool_pow, 1)
            factors(Step(0, 0))
            moments(Step(0, 1))
            pool.wait_ge(act_set, 4)
            pool.wait_ge(w2_done, 3)
            pool.tensor_tensor(w2_lo[:, TAPS:NW2], w2_raw[:, TAPS:NW2], w2_hi[:, TAPS:NW2].bitcast(f32), ALU.subtract).then_inc(sum_lo, 1)

            def body(i, front, norm):
                pool.wait_ge(ps_done, i.after(1, 1))
                past(pool, xcl_done, i.after(2, 0))
                for c in (1, 2):
                    pool.tensor_tensor(phases(xc, c), two(p_sum), phases(h[i.par()][:], c), ALU.add).then_inc(xs_done, 1)
                if front:
                    factors(i + 1)
                if norm:
                    moments(i + 2)
                for k in range(2 if front else 0):
                    pool.wait_ge(cand_done, i.after(2, k + 1))
                    pool.tensor_tensor(dif[k], h[i.par()][:, halves(k)], cand[k], ALU.subtract).then_inc(dif_done, 1)
                    pool.wait_ge(upd_done, i.after(2, k + 1))
                    pool.wait_ge(s_res[i.par()], i.load())
                    pool.tensor_tensor(res[i.par()][:, halves(k)], upd[k], res[i.par()][:, halves(k)], ALU.add).then_inc(y_done, 1)

            steps(pool, body)

        @block.scalar
        def _(act):
            def norm_evac(s):
                for k in range(2):
                    act.wait_ge(tr_done, s.after(2, k + 1))
                    act.activation(h[s.par()][:, halves(k)], bank[B_FRONT[k]][:], ACT.Relu).then_inc(h_done, 1)
                    act.activation(h_hi[s.par()][:, halves(k)], bank[B_FRONT[k]][:], ACT.Relu).then_inc(hh_done, 1)

            def conv1_evac(s):
                for k in range(2):
                    act.wait_ge(c1_mm, s.after(2, k + 1))
                    if k == 0:
                        past(act, ql_done, s.after(3, 0))
                        past(act, qh_done, s.after(3, 0))
                    act.activation(c1[:, 2 * k:2 * k + 2, PAD:PAD + N_NODE], bank[B_FRONT[k]][:].rearrange("p (b n) -> p b n", b=2),
                                   ACT.Relu, bias=bias_c[:, 0:1], scale=scale_c[:, 0:1]).then_inc(c1_act, 1)

            def msg_evac(s):
                for q, (t0, nt) in enumerate(MSG_LOTS):
                    act.wait_ge(ms_mm, s.after(3, q + 1))
                    v = bank[B_MSG[q]][:, 0:nt * MSGW].rearrange("p (t c) -> p t c", c=MSGW)
                    if q == 0:
                        past(act, pf, s.after(PF, 0))
                    act.activation(se[:, t0:t0 + nt, :], v[:, :, P:P + 3], ACT.Copy).then_inc(se_act, 1)
                    act.activation(msg[:, t0:t0 + nt, :], v[:, :, 0:P], ACT.Relu).then_inc(ms_act, 1)

            def factor_copy(s):
                act.wait_ge(ft_done, s.after(1, 1))
                past(act, di_mm, s.after(STEP_B, 0))
                for q in (2, 3):
                    last = act.activation(factor_rows(q), feat_t[32 * q:32 * q + 16], ACT.Copy)
                last.then_inc(fc_act, 1)

            def exps(s):
                for b in range(STEP_B):
                    act.wait_ge(di_mm, s.after(STEP_B, b + 1))
                    act.activation(aff[:, b, :], bank[B_DIST[b]][:], ACT.Exp).then_inc(exp_done, 1)

            def agg_evac(s):
                for k in range(2):
                    act.wait_ge(ag_mm, s.after(2, k + 1))
                    act.activation(agg_hi[:, halves(k)], bank[B_AGG[k]][:], ACT.Copy).then_inc(agh_done, 1)

            def quarter_hi(s, c):
                act.wait_ge(qd_done, s.after(3, c + 1))
                past(act, c2_mm, s.after(6, 2 * c - 4))
                act.activation(quart_hi[:, c, 0], odds(*half_seq(c), QROW), ACT.Copy)
                act.activation(flat(quart_hi[:, c, 1:3]), flat(quart_dif[:, c]),
                               ACT.Copy).then_inc(qh_done, 1)

            def pp_evac(i):
                act.wait_ge(c2_mm, i.after(6, 1))
                past(act, ps_done, i.after(1, 0))
                act.activation(pp[:], bank[B_PP][:, 0:HALF // 2], ACT.Copy).then_inc(pp_act, 1)

            def conv2_relu(i, k):
                act.wait_ge(yc_done, i.after(3, k + 2))
                act.activation(xc[:, halves(k)], xc[:, halves(k)], ACT.Relu, bias=bias_c[:, 1:2]).then_inc(xc_done, 1)

            def hidden_n(i, k):
                act.wait_ge(gn_mm, i.after(2, k + 1))
                past(act, upd_done, i.after(2, 0))
                act.activation(ghn[k], bank[B_GN][:], ACT.Identity, bias=bias_c[:, 5:6], scale=0.5).then_inc(gn_act, 1)

            def gate_tanh(i, k):
                act.wait_ge(g_mm, i.after(6, 3 * k + 1))
                act.activation(tr[k], bank[B_R][:], ACT.Tanh, bias=bias_c[:, 2:3], scale=0.5).then_inc(tr_act, 1)
                act.wait_ge(g_mm, i.after(6, 3 * k + 2))
                act.activation(tz[k], bank[B_Z][:], ACT.Tanh, bias=bias_c[:, 3:4], scale=0.5).then_inc(tz_act, 1)

            def cand_tanh(i, k):
                act.wait_ge(pre_done, i.after(2, k + 1))
                act.activation(cand[k], pre[k], ACT.Tanh, bias=bias_c[:, 4:5]).then_inc(cand_done, 1)

            z = Step(0, 0)
            act.wait_ge(s_w1, 16)
            act.activation(w1_hi[:], w1_raw[:], ACT.Copy).then_inc(act_set, 1)
            norm_evac(z)
            act.wait_ge(s_wg, 16)
            act.activation(wg_hi[:], wg_raw, ACT.Copy).then_inc(act_set, 1)
            msg_evac(z)
            act.wait_ge(dve_set, 5)
            conv1_evac(z)
            act.wait_ge(w2_done, 1)
            act.activation(w2_hi[:, 0:TAPS], w2_raw[:, 0:TAPS], ACT.Copy).then_inc(act_set, 1)
            act.wait_ge(w2_done, 3)
            act.activation(w2_hi[:, TAPS:NW2], w2_raw[:, TAPS:NW2], ACT.Copy).then_inc(act_set, 1)
            for c in range(3):
                quarter_hi(z, c)
            act.wait_ge(pool_pow, 3)
            factor_copy(z)
            exps(z)
            agg_evac(z)

            def body(i, front, norm):
                if front:
                    past(act, dif_done, i.after(2, 0))
                    norm_evac(i + 1)
                pp_evac(i)
                if front:
                    conv1_evac(i + 1)
                    msg_evac(i + 1)
                    quarter_hi(i + 1, 0)
                    quarter_hi(i + 1, 1)
                    factor_copy(i + 1)
                conv2_relu(i, 0)
                conv2_relu(i, 1)
                hidden_n(i, 0)
                if front:
                    quarter_hi(i + 1, 2)
                gate_tanh(i, 0)
                if front:
                    exps(i + 1)
                cand_tanh(i, 0)
                hidden_n(i, 1)
                gate_tanh(i, 1)
                cand_tanh(i, 1)
                if front:
                    agg_evac(i + 1)

            steps(act, body)

        @block.vector
        def _(dve):
            chain = [0]

            def link(ins):
                chain[0] += 1
                ins.then_inc(dve_set, 1)
                dve.wait_ge(dve_set, chain[0])

            def norm_stats(s):
                dve.wait_ge(s_x[s.par()], s.load())
                past(dve, pm, s.after(PM, 0))
                for t in range(TILES):
                    last = dve.bn_stats(stats[:, t, :], xt[s.par()][:, t, :])
                last.then_inc(st_done, 1)

            def norm_apply(s):
                dve.wait_ge(pm, s.after(PM, PM))
                for t in range(TILES):
                    last = dve.tensor_scalar(xt[s.par()][:, t, :], xt[s.par()][:, t, :], mean[:, t, :], rstd[:, t, :],
                                             ALU.subtract, ALU.mult)
                    if t % (TILES // 2) == TILES // 2 - 1:
                        last.then_inc(xn_done, 1)

            def norm_split(s):
                for k in range(2):
                    dve.wait_ge(hh_done, s.after(2, k + 1))
                    dve.tensor_tensor(h_lo[s.par()][:, halves(k)], h[s.par()][:, halves(k)],
                                      h_hi[s.par()][:, halves(k)].bitcast(f32), ALU.subtract).then_inc(hl_done, 1)

            def differences(s):
                dve.wait_ge(c1_act, s.after(2, 2))
                past(dve, qh_done, s.after(3, 0))
                dve.tensor_tensor(half_dif[:, :, :, 0:SROW - 1], evens(c1[:], 0, 1, SROW - 1), twice(odds(c1[:], 0, 1, SROW - 1)), ALU.subtract).then_inc(hd_done, 1)
                dve.wait_ge(hd_done, s.after(1, 1))
                for c in range(3):
                    dve.tensor_tensor(quart_dif[:, c], evens(*half_seq(c), QROW), twice(odds(*half_seq(c), QROW)),
                                      ALU.subtract).then_inc(qd_done, 1)

            def quarter_lo(s, c):
                dve.wait_ge(qh_done, s.after(3, c + 1))
                dve.tensor_tensor(quart_lo[:, c, 0], odds(*half_seq(c), QROW), quart_hi[:, c, 0].bitcast(f32), ALU.subtract)
                dve.tensor_tensor(flat(quart_lo[:, c, 1:3]), flat(quart_dif[:, c]), flat(quart_hi[:, c, 1:3]).bitcast(f32),
                                  ALU.subtract).then_inc(ql_done, 1)

            def factor_blocks(s):
                dve.wait_ge(pf, s.after(PF, PF))
                past(dve, fc_act, s.after(1, 0))
                past(dve, fc_dve, s.after(1, 0))
                dve.transpose(feat_t[:].rearrange("p t s f -> p (t s f)"), feat[:].rearrange("p t s f -> p (t s f)")).then_inc(ft_done, 1)
                dve.wait_ge(ft_done, s.after(1, 1))
                past(dve, di_mm, s.after(STEP_B, 0))
                for q in (0, 1):
                    last = dve.tensor_copy(factor_rows(q), feat_t[32 * q:32 * q + 16])
                last.then_inc(fc_dve, 1)

            def own_p(c):
                at = (c % 2) * (HALF // 2)
                return twice(bank[B_PP][:, at:at + HALF // 2])

            def p_combine(i):
                dve.wait_ge(pp_act, i.after(1, 1))
                dve.wait_ge(c2_mm, i.after(6, 2))
                past(dve, xs_done, i.after(2, 0))
                dve.tensor_tensor(two(p_sum), twice(pp[:]), two(bank[B_PR[0]][:]), ALU.add).then_inc(ps_done, 1)

            def combine_own(i, c):
                dve.wait_ge(c2_mm, i.after(6, 2 * c + 1))
                dve.wait_ge(xs_done, i.after(2, c))
                dve.tensor_tensor(phases(xc, c), phases(xc, c), own_p(c), ALU.add).then_inc(qs_done, 1)

            def combine(i, c):
                dve.wait_ge(c2_mm, i.after(6, 2 * c + 2))
                dve.wait_ge(qs_done, i.after(2, c))
                for at in ([slice(0, QB)], [slice(0, QB // 2), slice(QB // 2, QB)])[c - 1]:
                    dve.tensor_tensor(phases(xc, c)[:, :, at], phases(xc, c)[:, :, at], two(bank[B_PR[c]][:])[:, :, at],
                                      ALU.add).then_inc(yc_done, 1)

            def masks(s):
                dve.wait_ge(s_mask, s.after(16, 16))
                for b in range(STEP_B):
                    dve.wait_ge(exp_done, s.after(STEP_B, b + 1))
                    dve.tensor_tensor(aff[:, b, :], aff[:, b, :], mask[:, b, :], ALU.mult).then_inc(aff_done, 1)

            def agg_split(s):
                for k in range(2):
                    dve.wait_ge(agh_done, s.after(2, k + 1))
                    dve.tensor_tensor(agg_lo[:, halves(k)], bank[B_AGG[k]][:], agg_hi[:, halves(k)].bitcast(f32),
                                      ALU.subtract).then_inc(agl_done, 1)

            def conv2_split(i, k):
                dve.wait_ge(xc_done, i.after(2, k + 1))
                dve.tensor_copy(xc_hi[:, halves(k)], xc[:, halves(k)]).then_inc(xch_done, 1)
                dve.wait_ge(xch_done, i.after(2, k + 1))
                dve.tensor_tensor(xc_lo[:, halves(k)], xc[:, halves(k)], xc_hi[:, halves(k)].bitcast(f32),
                                  ALU.subtract).then_inc(xcl_done, 1)

            def candidate(i, k):
                dve.wait_ge(tr_act, i.after(2, k + 1))
                dve.scalar_tensor_tensor(rg[k], tr[k], 1.0, ghn[k], ALU.add, ALU.mult).then_inc(rg_done, 1)
                dve.wait_ge(rg_done, i.after(2, k + 1))
                dve.wait_ge(g_mm, i.after(6, 3 * k + 3))
                dve.tensor_tensor(pre[k], rg[k], bank[B_IN][:], ALU.add).then_inc(pre_done, 1)

            def update(i, k, last):
                if last:
                    dve.wait_ge(cand_done, i.after(2, k + 1))
                    dve.tensor_tensor(dif[k], h[i.par()][:, halves(k)], cand[k], ALU.subtract).then_inc(dif_done, 1)
                dve.wait_ge(dif_done, i.after(2, k + 1))
                dve.wait_ge(tz_act, i.after(2, k + 1))
                dve.scalar_tensor_tensor(zd[k], tz[k], 1.0, dif[k], ALU.add, ALU.mult).then_inc(zd_done, 1)
                dve.wait_ge(zd_done, i.after(2, k + 1))
                past(dve, y_done, i.after(2, 0))
                dve.scalar_tensor_tensor(upd[k], zd[k], 0.5, cand[k], ALU.mult, ALU.add).then_inc(upd_done, 1)
                if last:
                    dve.wait_ge(upd_done, i.after(2, k + 1))
                    dve.wait_ge(s_res[i.par()], i.load())
                    dve.tensor_tensor(res[i.par()][:, halves(k)], upd[k], res[i.par()][:, halves(k)], ALU.add).then_inc(y_done, 1)

            z = Step(0, 0)
            dve.memset(ones[:].bitcast(f32), 1.0)
            dve.memset(bias_msg[:].bitcast(f32), 0.0)
            dve.memset(c1[:], 0.0).then_inc(dve_fill, 1)
            norm_stats(z)
            dve.wait_ge(act_set, 1)
            dve.tensor_tensor(w1_lo[:], w1_raw[:], w1_hi[:].bitcast(f32), ALU.subtract).then_inc(w_ready, 1)
            dve.wait_ge(s_row, 16)
            dve.tensor_copy(mrow_hi[:], mrow[:]).then_inc(dve_fill, 1)
            dve.wait_ge(dve_fill, 2)
            for t in range(3):
                at = slice(t * MSGW, (t + 1) * MSGW)
                dve.tensor_copy(bias_msg[0:1, at], mrow_hi[0:1, :].bitcast(f32))
                last = dve.tensor_tensor(bias_msg[32:33, at], mrow[32:33, :], mrow_hi[32:33, :].bitcast(f32), ALU.subtract)
            last.then_inc(w_ready, 1)
            norm_apply(z)
            dve.wait_ge(s_vec, 16)
            dve.wait_ge(pool_pow, 2)
            link(dve.tensor_tensor(scale_c[:], scale_c[:], vcol[:, V_G1:V_G2 + 1:4], ALU.mult))
            dve.tensor_copy(scale_w[:], scale_c[:, 1:2].to_broadcast([P, P])).then_inc(w2_scale, 1)
            link(dve.tensor_tensor(tmp_c[:], scale_c[:], vcol[:, V_M1:V_M2 + 1:4], ALU.mult))
            link(dve.tensor_tensor(bias_c[:, 0:2], vcol[:, V_B1:V_B2 + 1:4], tmp_c[:], ALU.subtract))
            link(dve.tensor_tensor(bias_c[:, 2:4], vcol[:, V_IR:V_IZ + 1], vcol[:, V_HR:V_HZ + 1], ALU.add))
            dve.tensor_copy(bias_c[:, 4:5], vcol[:, V_IN:V_IN + 1])
            dve.tensor_scalar(bias_c[:, 5:6], vcol[:, V_HN:V_HN + 1], 0.5, None, ALU.mult)
            link(dve.tensor_scalar(bias_c[:, 2:4], bias_c[:, 2:4], 0.5, None, ALU.mult))
            norm_split(z)
            taps = w2_raw[:, 0:TAPS]

            def tap(b):
                return w2_raw[:, b:b + 13:4]

            def sums(k):
                return w2_raw[:, TAPS + 4 * k:TAPS + 4 * k + 4]
            dve.wait_ge(s_w2, 16)
            dve.wait_ge(w2_scale, 2)
            dve.tensor_tensor(taps, taps, bank[B_IN][:, 0:P].unsqueeze(1).to_broadcast([P, TAPS, P]), ALU.mult).then_inc(w2_done, 1)
            dve.wait_ge(w2_done, 1)
            dve.tensor_tensor(sums(1), tap(0), tap(1), ALU.add)
            dve.tensor_tensor(sums(3), tap(0), tap(2), ALU.add)
            dve.tensor_tensor(sums(4), tap(1), tap(3), ALU.add)
            dve.tensor_tensor(sums(2), tap(2), tap(3), ALU.add).then_inc(w2_done, 1)
            dve.wait_ge(w2_done, 2)
            dve.tensor_tensor(sums(0), sums(1), sums(2), ALU.add).then_inc(w2_done, 1)
            norm_stats(z + 1)
            differences(z)
            dve.wait_ge(pool_pow, 3)
            factor_blocks(z)
            dve.wait_ge(act_set, 3)
            dve.tensor_tensor(w2_lo[:, 0:TAPS], taps, w2_hi[:, 0:TAPS].bitcast(f32), ALU.subtract).then_inc(w_ready, 1)
            norm_apply(z + 1)
            masks(z)
            for c in range(3):
                quarter_lo(z, c)
            dve.wait_ge(act_set, 2)
            dve.tensor_tensor(wg_lo[:], wg_raw, wg_hi[:].bitcast(f32), ALU.subtract).then_inc(w_ready, 1)
            agg_split(z)

            def body(i, front, norm_on):
                if front:
                    norm_split(i + 1)
                p_combine(i)
                if norm_on:
                    norm_stats(i + 2)
                if front:
                    differences(i + 1)
                combine_own(i, 1)
                combine(i, 1)
                if front:
                    factor_blocks(i + 1)
                combine_own(i, 2)
                if front:
                    quarter_lo(i + 1, 0)
                combine(i, 2)
                if front:
                    quarter_lo(i + 1, 1)
                conv2_split(i, 0)
                conv2_split(i, 1)
                if front:
                    quarter_lo(i + 1, 2)
                candidate(i, 0)
                if front:
                    masks(i + 1)
                update(i, 0, not front)
                candidate(i, 1)
                if norm_on:
                    norm_apply(i + 2)
                update(i, 1, not front)
                if front:
                    agg_split(i + 1)

            steps(dve, body)

        @block.tensor
        def _(pe):
            def mm(out_, w, x, start, stop):
                return pe.matmul(out_, w, x, start=start, stop=stop)

            def products(terms):
                return [(w, x) for (wh, wl), (xh, xl) in terms for w, x in ((wh, xh), (wh, xl), (wl, xh))]

            def group(out_, terms, extra=()):
                pairs = list(extra) + products(terms)
                for q, (w, x) in enumerate(pairs):
                    last = mm(out_, w, x, q == 0, q == len(pairs) - 1)
                return last

            def transpose_x(s):
                for k in range(2):
                    pe.wait_ge(xn_done, s.after(2, k + 1))
                    for t in range(TILES // 2):
                        last = pe.transpose(bank[B_FRONT[k]][:, t * P:(t + 1) * P], xt[s.par()][:, k * TILES // 2 + t, :], ident[:])
                    last.then_inc(tr_done, 1)

            def conv1(s):
                p = s.par()
                pe.wait_ge(hl_done, s.after(2, 2))
                for k in range(2):
                    group(bank[B_FRONT[k]][:], [((w1_hi[:], w1_lo[:]), (h_hi[p][:, halves(k)], h_lo[p][:, halves(k)]))])\
                        .then_inc(c1_mm, 1)

            def messages(s):
                for q, (t0, nt) in enumerate(MSG_LOTS):
                    mm(bank[B_MSG[q]][:, 0:nt * MSGW], ones[:, 0:P], bias_msg[:, 0:nt * MSGW], True, False)
                    for t in range(nt):
                        last = mm(bank[B_MSG[q]][:, t * MSGW:(t + 1) * MSGW], h[s.par()][:, (t0 + t) * P:(t0 + t + 1) * P],
                                  wm_sb[:], False, t == nt - 1)
                    last.then_inc(ms_mm, 1)

            def distances(s):
                pe.wait_ge(fc_act, s.after(1, 1))
                pe.wait_ge(fc_dve, s.after(1, 1))
                for b in range(STEP_B):
                    for m in range(MT):
                        at = b * N_NODE
                        last = mm(bank[B_DIST[b]][:, m * N_NODE:(m + 1) * N_NODE], factor[:, 0, at + m * P:at + (m + 1) * P],
                                  factor[:, 1, at:at + N_NODE], True, True)
                    last.then_inc(di_mm, 1)

            def aggregate(s, before=None):
                pe.wait_ge(exp_done, s.after(STEP_B, STEP_B))
                for b in range(STEP_B):
                    if b == 2 and before:
                        pe.wait_ge(tz_act, before.after(2, 2))
                    pe.wait_ge(aff_done, s.after(STEP_B, b + 1))
                    for m in range(MT):
                        last = mm(bank[B_AGG[b // 2]][:, (b % 2) * N_NODE:(b % 2 + 1) * N_NODE], msg[:, b * MT + m, :],
                                  aff[:, b, m * N_NODE:(m + 1) * N_NODE], m == 0, m == MT - 1)
                    if b % 2:
                        last.then_inc(ag_mm, 1)

            def weights(c, d, t):
                at = {(0, 0): TAPS, (0, 1): TAPS + 4, (0, 2): TAPS + 8, (1, 0): TAPS + 12, (2, 0): TAPS + 16}.get((c, d))
                if t == 4:
                    at = TAPS - 1
                elif at is None:
                    at = 4 * t + (c - 1) + 2 * (d - 1)
                else:
                    at += t
                return w2_hi[:, at, :], w2_lo[:, at, :]

            def wide(c, d):
                if d:
                    o = bank[B_PR[c]][:, (d - 1) * HALF // 2:d * HALF // 2]
                else:
                    o = bank[B_PP][:, (c % 2) * HALF // 2:(c % 2 + 1) * HALF // 2]
                taps = range(5 if c < 2 and d < 2 else 4)
                return group(o.rearrange("p (b v) -> p b v", b=STEP_B),
                             [(weights(c, d, t), (quart_hi[:, c, d, :, t:t + QN], quart_lo[:, c, d, :, t:t + QN])) for t in taps])

            def conv2_p(i):
                pe.wait_ge(ql_done, i.after(3, 3))
                pe.wait_ge(exp_done, i.after(STEP_B, STEP_B))
                wide(0, 0).then_inc(c2_mm, 1)
                wide(0, 1)
                wide(0, 2).then_inc(c2_mm, 1)

            def conv2_q(i):
                pe.wait_ge(pp_act, i.after(1, 1))
                wide(1, 0).then_inc(c2_mm, 1)
                wide(1, 1)
                wide(1, 2).then_inc(c2_mm, 1)

            def conv2_r(i):
                pe.wait_ge(qs_done, i.after(2, 1))
                wide(2, 0).then_inc(c2_mm, 1)
                pe.wait_ge(ps_done, i.after(1, 1))
                wide(2, 1)
                wide(2, 2).then_inc(c2_mm, 1)

            def part(b, terms, first, last_):
                pairs = products(terms)
                for q, (w, x) in enumerate(pairs):
                    last = mm(bank[b][:], w, x, first and q == 0, last_ and q == len(pairs) - 1)
                return last

            def gates(i, k, front):
                p = i.par()
                hid = (h_hi[p][:, halves(k)], h_lo[p][:, halves(k)])
                con = (xc_hi[:, halves(k)], xc_lo[:, halves(k)])
                agg = (agg_hi[:, halves(k)], agg_lo[:, halves(k)])

                def w(src, gate):
                    return wg_hi[:, src, gate * P:(gate + 1) * P], wg_lo[:, src, gate * P:(gate + 1) * P]
                if k:
                    pe.wait_ge(tr_act, i.after(2, 1))
                part(B_R, [(w(0, 0), hid), (w(2, 0), agg)], True, False)
                if k:
                    pe.wait_ge(tz_act, i.after(2, 1))
                part(B_Z, [(w(0, 1), hid), (w(2, 1), agg)], True, False)
                if k:
                    pe.wait_ge(gn_act, i.after(2, 1))
                part(B_GN, [(w(0, 2), hid)], True, True).then_inc(gn_mm, 1)
                if k:
                    pe.wait_ge(pre_done, i.after(2, 1))
                else:
                    past(pe, pre_done, i.after(2, 0))
                part(B_IN, [(w(2, 2), agg)], True, False)
                if k == 0 and front:
                    pe.wait_ge(yc_done, i.after(3, 3))
                    distances(i + 1)
                pe.wait_ge(xcl_done, i.after(2, k + 1))
                part(B_R, [(w(1, 0), con)], False, True).then_inc(g_mm, 1)
                part(B_Z, [(w(1, 1), con)], False, True).then_inc(g_mm, 1)
                part(B_IN, [(w(1, 2), con)], False, True).then_inc(g_mm, 1)

            z = Step(0, 0)
            pe.wait_ge(pool_set, 3)
            transpose_x(z)
            pe.wait_ge(w2_scale, 1)
            pe.transpose(bank[B_IN][:, 0:P], scale_w[:], ident[:]).then_inc(w2_scale, 1)
            pe.wait_ge(s_wm, 16)
            pe.wait_ge(w_ready, 2)
            pe.wait_ge(hh_done, 2)
            messages(z)
            conv1(z)
            pe.wait_ge(c1_act, z.after(2, 2))
            distances(z)
            aggregate(z)
            pe.wait_ge(w_ready, 4)
            pe.wait_ge(sum_lo, 1)

            def body(i, front, norm):
                if front:
                    transpose_x(i + 1)
                conv2_p(i)
                if front:
                    conv1(i + 1)
                    past(pe, pre_done, i.after(2, 0))
                pe.wait_ge(agl_done, i.after(2, 2))
                if front:
                    messages(i + 1)
                    pe.wait_ge(c1_act, (i + 1).after(2, 2))
                conv2_q(i)
                conv2_r(i)
                if front:
                    pe.wait_ge(ms_act, (i + 1).after(3, 3))
                gates(i, 0, front)
                gates(i, 1, front)
                if front:
                    pe.wait_ge(tr_act, i.after(2, 2))
                    aggregate(i + 1, i)

            steps(pe, body)


_VECTORS = ["bn1_g", "bn1_b", "bn1_m", "bn1_v", "bn2_g", "bn2_b", "bn2_m", "bn2_v"]


def kernel(**inputs):
    import numpy as np
    import concourse.bacc as bacc
    from concourse import mybir
    from concourse.bass_utils import run_bass_kernel_spmd

    a = {k.replace("L0_gnn_", ""): np.asarray(v) for k, v in inputs.items()}
    x, adj = a["x"], a["adj"]
    vectors = np.concatenate([np.stack([a[n] for n in _VECTORS]), a["b_ih"].reshape(3, P), a["b_hh"].reshape(3, P)])
    w_ih, w_hh = a["w_ih"], a["w_hh"]
    arrays = {
        "x_tok": x.reshape(STEPS, TILES, P, P).transpose(0, 2, 1, 3),
        "x_chan": x.reshape(STEPS, STEP_TOK, P).transpose(0, 2, 1),
        "mask_t": adj.transpose(0, 2, 1).reshape(STEPS, STEP_B, MT, P, N_NODE).transpose(0, 3, 1, 2, 4).reshape(STEPS, P, STEP_B, HALF),
        "vec_col": vectors.T,
        "msg_row": np.concatenate([a["b_msg"], a["b_se"], np.zeros(1, np.float32)]).reshape(1, MSGW),
        "w1": a["conv1_w"][:, :, 0].T,
        "w2": a["conv2_w"].transpose(1, 2, 0),
        "wg": np.stack([w_hh.T, w_ih[:, :P].T, w_ih[:, P:].T], axis=1),
        "wm": np.concatenate([a["w_msg"].T, a["w_se"].T, np.zeros((P, 1), np.float32)], axis=1),
    }
    arrays = {k: np.ascontiguousarray(v) for k, v in arrays.items()}
    nc = bacc.Bacc("TRN2", target_bir_lowering=False, num_devices=1)
    args = [nc.dram_tensor(n, v.shape, mybir.dt.from_np(v.dtype), kind="ExternalInput").ap() for n, v in arrays.items()]
    out = nc.dram_tensor("out", (STEPS, P, STEP_TOK), mybir.dt.float32, kind="ExternalOutput").ap()
    gnn_layer(nc, *args, out)
    r = run_bass_kernel_spmd(nc, [arrays], core_ids=[0])
    return r.results[0]["out"].transpose(0, 2, 1).reshape(N_BATCH, N_NODE, P)
```

```python
import concourse.bass as bass
from concourse import mybir
from contextlib import ExitStack

P = 128
N_BATCH, N_NODE = 32, 256
STEP_B = 4
STEP_TOK = STEP_B * N_NODE
STEPS = N_BATCH // STEP_B
TILES = STEP_TOK // P
HALF = 512
MT = N_NODE // P
TAPS, PAD = 17, 8
ROW = N_NODE + 2 * PAD + 4
QN = N_NODE // 4
QB = STEP_B * QN
QROW = QN + 4
SROW = 2 * QROW + 2
NW2 = TAPS + 20
MSGW = P + 4
EPS = 1e-5
(V_G1, V_B1, V_M1, V_V1, V_G2, V_B2, V_M2, V_V2, V_IR, V_IZ, V_IN, V_HR, V_HZ, V_HN) = range(14)
NVEC = 14
PF, PM = 6, 5


def gnn_layer(nc, x_tok, x_chan, mask_t, vec_col, msg_row, w1, w2, wg, wm, out):
    f32, f32r = mybir.dt.float32, mybir.dt.float32r
    ALU, ACT = mybir.AluOpType, mybir.ActivationFunctionType
    ctx = ExitStack()
    with ctx:
        def sb(name, shape, dt=f32):
            return ctx.enter_context(nc.sbuf_tensor(name, shape, dt))

        def sem(name):
            return ctx.enter_context(nc.semaphore(name))

        vcol = sb("vcol", [P, NVEC])
        mrow = sb("mrow", [P, MSGW])
        aff = sb("aff", [P, 2, HALF])
        mask = sb("mask", [P, STEP_B, HALF])
        w1_raw = aff[:, 1, 0:P]
        back = sb("back", [P, (NW2 + 9) * P])
        w2_raw = back[:, 0:NW2 * P].rearrange("p (t c) -> p t c", c=P)
        wg_raw = back[:, NW2 * P:(NW2 + 9) * P].rearrange("p (s c) -> p s c", s=3)
        wm_sb = sb("wm_sb", [P, MSGW])
        w1_hi, w1_lo = sb("w1_hi", [P, P], f32r), sb("w1_lo", [P, P], f32r)
        w2_hi, w2_lo = sb("w2_hi", [P, NW2, P], f32r), sb("w2_lo", [P, NW2, P], f32r)
        wg_hi, wg_lo = sb("wg_hi", [P, 3, 3 * P], f32r), sb("wg_lo", [P, 3, 3 * P], f32r)
        ident = sb("ident", [P, P])
        ones = sb("ones", [P, P], f32r)
        ones32 = sb("ones32", [P, 3 * TILES])
        scale_c = sb("scale_c", [P, 2])
        bias_c = sb("bias_c", [P, 6])
        tmp_c = sb("tmp_c", [P, 2])
        minus_half = sb("minus_half", [P, TILES])
        minus_one, quarter = sb("minus_one", [P, TILES]), sb("quarter", [P, TILES])
        bias_msg = sb("bias_msg", [P, 3 * MSGW], f32r)
        xt = [sb(f"xt{k}", [P, TILES, P]) for k in range(2)]
        stats = sb("stats", [P, TILES, 6])
        mo_sum, mo_dif, mo_dev, mo_sq, mean, rstd = (
            sb(n, [P, TILES, 1]) for n in ("mo_sum", "mo_dif", "mo_dev", "mo_sq", "mean", "rstd"))
        h = [sb(f"h{k}", [P, STEP_TOK]) for k in range(2)]
        h_hi = [sb(f"h_hi{k}", [P, STEP_TOK], f32r) for k in range(2)]
        h_lo = [sb(f"h_lo{k}", [P, STEP_TOK], f32r) for k in range(2)]
        c1 = sb("c1", [P, STEP_B, ROW])
        half_dif = sb("half_dif", [P, 2, STEP_B, SROW])
        quart_dif = sb("quart_dif", [P, 3, 2, STEP_B, QROW])
        quart_hi = sb("quart_hi", [P, 3, 3, STEP_B, QROW], f32r)
        quart_lo = sb("quart_lo", [P, 3, 3, STEP_B, QROW], f32r)
        msg = sb("msg", [P, TILES, P])
        msg_hi, msg_lo = sb("msg_hi", [P, TILES, P], f32r), sb("msg_lo", [P, TILES, P], f32r)
        se = sb("se", [P, TILES, 3])
        se_hi = sb("se_hi", [P, TILES, 3], f32r)
        sq_el = sb("sq_el", [P, TILES, 3])
        sq, sq_a = sb("sq", [P, TILES, 1]), sb("sq_a", [P, TILES, 1])
        nsq_hi = sb("nsq_hi", [P, TILES, 1], f32r)
        se_parts = sb("se_parts", [P, TILES, 2, 3])
        feat = sb("feat", [P, TILES, 2, 32])
        feat_t = aff[:, 0, :].rearrange("p (t s f) -> p t s f", s=2, f=32)
        factor = sb("factor", [P, 2, STEP_TOK], f32r)
        aff_hi, aff_lo = sb("aff_hi", [P, STEP_B, HALF], f32r), sb("aff_lo", [P, STEP_B, HALF], f32r)
        agg_hi, agg_lo = sb("agg_hi", [P, STEP_TOK], f32r), sb("agg_lo", [P, STEP_TOK], f32r)
        xc = back[:, 0:STEP_TOK]
        res = xc
        tr, tz, cand, dif = ([back[:, (2 + 2 * q + k) * HALF:(3 + 2 * q + k) * HALF] for k in range(2)] for q in range(4))
        ghn = cand
        rg = pre = tr
        zd = upd = dif
        p_sum = back[:, 10 * HALF:11 * HALF]
        pp = back[:, 11 * HALF:11 * HALF + HALF // 2]
        xc_hi, xc_lo = sb("xc_hi", [P, STEP_TOK], f32r), sb("xc_lo", [P, STEP_TOK], f32r)
        mrow_hi = xc_hi[:, 0:MSGW]
        bank = [ctx.enter_context(nc.psum_tensor(f"bank{k}", [P, HALF], f32)) for k in range(8)]
        B_PR = (0, 3, 0)
        B_PP = 1
        B_FRONT = (2, 3)
        B_MSG = (4, 5, 6)
        B_R, B_Z, B_GN, B_IN = 4, 5, 6, 7
        B_DIST = (2, 3, 0, 1)
        B_AGG = (4, 5)
        MSG_LOTS = [(0, 3), (3, 3), (6, 2)]

        s_vec, s_row, s_w1, s_w2, s_wg, s_wm = (sem(n) for n in ("s_vec", "s_row", "s_w1", "s_w2", "s_wg", "s_wm"))
        s_x = [sem(f"s_x{k}") for k in range(2)]
        s_mask, s_res = sem("s_mask"), sem("s_res")
        s_out = [sem(f"s_out{k}") for k in range(2)]
        pool_set = sem("pool_set")
        act_set = sem("act_set")
        dve_fill = sem("dve_fill")
        w2_done = sem("w2_done")
        sum_lo = sem("sum_lo")
        pool_sums = sem("pool_sums")
        pool_pow = sem("pool_pow")
        dve_set = sem("dve_set")
        w_ready = sem("w_ready")
        st_done = sem("st_done")
        moment_chain = sem("moment_chain")
        xn_done = sem("xn_done")
        tr_done = sem("tr_done")
        hh_done, hl_done = sem("hh_done"), sem("hl_done")
        c1_mm, c1_act = sem("c1_mm"), sem("c1_act")
        hd_done, qd_done, qh_done, ql_done = sem("hd_done"), sem("qd_done"), sem("qh_done"), sem("ql_done")
        ms_mm, ms_act, se_act, ml_done = sem("ms_mm"), sem("ms_act"), sem("se_act"), sem("ml_done")
        factor_chain = sem("factor_chain")
        ft_done, fc_dve, fc_act = sem("ft_done"), sem("fc_dve"), sem("fc_act")
        di_mm, exp_done, aff_done = sem("di_mm"), sem("exp_done"), sem("aff_done")
        afh_done, afl_done = sem("afh_done"), sem("afl_done")
        ag_mm, agh_done, agl_done = sem("ag_mm"), sem("agh_done"), sem("agl_done")
        c2_mm = sem("c2_mm")
        pp_act, ps_done, qs_done, yc_done = sem("pp_act"), sem("ps_done"), sem("qs_done"), sem("yc_done")
        xs_done, xc_done, xch_done, xcl_done = sem("xs_done"), sem("xc_done"), sem("xch_done"), sem("xcl_done")
        g_mm = sem("g_mm")
        gn_mm, gn_act = sem("gn_mm"), sem("gn_act")
        tr_act, tz_act, rg_done, pre_done, cand_done = (
            sem(n) for n in ("tr_act", "tz_act", "rg_done", "pre_done", "cand_done"))
        dif_done, zd_done, upd_done, y_done, fin_done = (
            sem(n) for n in ("dif_done", "zd_done", "upd_done", "y_done", "fin_done"))

        class Step:
            def __init__(self, j, c):
                self.j, self.c = j, c

            def __add__(self, d):
                return Step(self.j, self.c + d)

            def par(self):
                return self.c % 2

            def n(self):
                return self.j * 2 + self.c

            def after(self, per, k):
                return self.j * (2 * per) + (self.c * per + k)

            def load(self):
                return self.j * 16 + 16 * (self.c // 2 + 1)

        def steps(eng, body):
            end = (STEPS - 2) // 2
            body(Step(0, 0), True, True, True)
            with eng.Fori(1, end) as j:
                body(Step(j, -1), True, True, True)
                body(Step(j, 0), True, True, True)
            body(Step(end - 1, 1), True, True, False)
            body(Step(end, 0), True, False, False)
            body(Step(end, 1), False, False, False)

        def past(eng, semaphore, value):
            if not isinstance(value, int) or value > 0:
                eng.wait_ge(semaphore, value)

        def halves(k):
            return slice(k * HALF, (k + 1) * HALF)

        def half_seq(c):
            return (c1[:], 1, 2) if c == 0 else (half_dif[:, c - 1], 0, 1)

        def evens(x, first, step, n):
            return bass.AP(x.tensor, x.offset + first, [x.ap[0], [2 * step, 2], x.ap[-2], [2 * step, n]])

        def odds(x, first, step, n):
            return bass.AP(x.tensor, x.offset + first + step, [x.ap[0], x.ap[-2], [2 * step, n]])

        def twice(x):
            return x.unsqueeze(1).to_broadcast([P, 2] + list(x.shape[1:]))

        def flat(x):
            return x.rearrange("p a b v -> p (a b v)")

        def factor_rows(q):
            return factor[0:16].rearrange("f s (t q j) -> f t s q j", q=4, j=32)[:, :, :, q, :]

        def phases(x, c):
            return x.rearrange("p (t f) -> p f t", f=4)[:, c - 1:4:2]

        def tap(b):
            return w2_raw[:, b:b + 13:4]

        def sums(k):
            return w2_raw[:, TAPS + 4 * k:TAPS + 4 * k + 4]

        def two(x):
            return x.rearrange("p (f n) -> p f n", f=2)

        block = ctx.enter_context(nc.Block())

        @block.sync
        def _(sp):
            def load_x(s):
                sp.dma_start(xt[s.par()][:], x_tok[bass.ds(s.n(), 1)].rearrange("o p t c -> p (o t) c"))\
                    .then_inc(s_x[s.par()], 16)

            def load_mask(s):
                sp.dma_start(mask[:], mask_t[bass.ds(s.n(), 1)].rearrange("o p b n -> p (o b) n")).then_inc(s_mask, 16)

            def load_res(s):
                sp.dma_start(res, x_chan[bass.ds(s.n(), 1)].rearrange("o p t -> p (o t)")).then_inc(s_res, 16)

            first = Step(0, 0)
            load_x(first)
            sp.dma_start(w1_raw, w1).then_inc(s_w1, 16)
            sp.dma_start(vcol[:], vec_col).then_inc(s_vec, 16)
            sp.dma_start(mrow[:], msg_row.to_broadcast([P, MSGW])).then_inc(s_row, 16)
            sp.dma_start(wm_sb[:], wm).then_inc(s_wm, 16)
            sp.dma_start(w2_raw[:, 0:TAPS], w2).then_inc(s_w2, 16)
            load_x(first + 1)
            sp.dma_start(wg_raw, wg).then_inc(s_wg, 16)
            load_mask(first)
            sp.wait_ge(tr_done, first.after(2, 2))
            load_x(first + 2)

            def body(i, front, norm, far):
                if front:
                    sp.wait_ge(afl_done, i.after(STEP_B, STEP_B))
                    load_mask(i + 1)
                if far:
                    sp.wait_ge(tr_done, (i + 1).after(2, 2))
                    load_x(i + 3)
                sp.wait_ge(xcl_done, i.after(2, 2))
                load_res(i)
                for k in range(2):
                    sp.wait_ge(y_done, i.after(2, k + 1))
                    sp.dma_start(out[bass.ds(i.n(), 1), :, halves(k)].rearrange("o p t -> p (o t)"), upd[k])\
                        .then_inc(s_out[k], 16)

            steps(sp, body)
            for k in range(2):
                sp.wait_ge(s_out[k], 16 * STEPS)

        @block.gpsimd
        def _(pool):
            chain = [0]

            def link(ins):
                chain[0] += 1
                ins.then_inc(pool_set, 1)
                pool.wait_ge(pool_set, chain[0])

            pool.memset(minus_half[:], -0.5)
            pool.memset(quarter[:], 0.25)
            pool.memset(minus_one[:], -1.0)
            pool.memset(ones32[:], 1.0)
            pool.memset(feat[:], 0.0)
            link(pool.memset(ident[:], 0.0))
            link(pool.affine_select(out=ident[:], in_=ident[:], compare_op=ALU.not_equal, fill=1.0, base=0,
                                    pattern=[[-1, P]], channel_multiplier=1))
            pool.memset(feat[:, :, 0, 12:14], 1.0)
            link(pool.memset(feat[:, :, 1, 14:16], 1.0))
            one3 = ones32[:, 0:3 * TILES].rearrange("p (t c) -> p t c", c=3)
            minus_one1, quarter1 = minus_one[:].unsqueeze(2), quarter[:].unsqueeze(2)

            def factors(s):
                g = [0]

                def done(ins):
                    g[0] += 1
                    ins.then_inc(factor_chain, 1)
                    pool.wait_ge(factor_chain, s.after(PF, g[0]))
                past(pool, ft_done, s.after(1, 0))
                pool.wait_ge(se_act, s.after(3, 3))
                pool.tensor_tensor(se_hi[:], se[:], one3, ALU.mult)
                done(pool.tensor_tensor(sq_el[:], se[:], se[:], ALU.mult))
                pool.tensor_tensor(se_parts[:, :, 1, :], se[:], se_hi[:].bitcast(f32), ALU.subtract)
                pool.tensor_scalar(se_parts[:, :, 0, :], se_hi[:].bitcast(f32), 1.0, 0.0, ALU.mult, ALU.add)
                done(pool.tensor_tensor(sq_a[:], sq_el[:, :, 0:1], sq_el[:, :, 1:2], ALU.add))
                done(pool.tensor_tensor(sq[:], sq_a[:], sq_el[:, :, 2:3], ALU.add))
                pool.tensor_tensor(nsq_hi[:], sq[:], minus_one1, ALU.mult)
                pt = se_parts[:].rearrange("p t a c -> p t (a c)")
                for r in range(2):
                    pool.tensor_scalar(feat[:, :, 0, 6 * r:6 * r + 6], pt, 1.0, 0.0, ALU.mult, ALU.add)
                    pool.tensor_scalar(feat[:, :, 1, 6 * r:3 + 6 * r], se_parts[:, :, r, :], 2.0, 0.0, ALU.mult, ALU.add)
                    last = pool.tensor_scalar(feat[:, :, 1, 3 + 6 * r:6 + 6 * r], se_parts[:, :, 1 - r, :], 2.0, 0.0,
                                              ALU.mult, ALU.add)
                done(last)
                pool.tensor_tensor(sq_a[:], sq[:], nsq_hi[:].bitcast(f32), ALU.add)
                pool.tensor_scalar(feat[:, :, 0, 14:15], nsq_hi[:].bitcast(f32), 1.0, 0.0, ALU.mult, ALU.add)
                done(pool.tensor_scalar(feat[:, :, 1, 12:13], nsq_hi[:].bitcast(f32), 1.0, 0.0, ALU.mult, ALU.add))
                pool.tensor_tensor(feat[:, :, 0, 15:16], sq_a[:], minus_one1, ALU.mult)
                pool.tensor_scalar(feat[:, :, 1, 13:14], sq_a[:], -1.0, 0.0, ALU.mult, ALU.add).then_inc(factor_chain, 1)

            def message_lo(s):
                pool.wait_ge(ms_act, s.after(3, 3))
                pool.tensor_tensor(msg_lo[:], msg[:], msg_hi[:].bitcast(f32), ALU.subtract).then_inc(ml_done, 1)

            def moments(s):
                g = [0]

                def done(ins):
                    g[0] += 1
                    ins.then_inc(moment_chain, 1)
                    pool.wait_ge(moment_chain, s.after(PM, g[0]))
                past(pool, xn_done, s.after(2, 0))
                pool.wait_ge(st_done, s.after(1, 1))
                pool.tensor_tensor(mo_sum[:], stats[:, :, 1:2], stats[:, :, 4:5], ALU.add)
                pool.tensor_tensor(mo_dif[:], stats[:, :, 1:2], stats[:, :, 4:5], ALU.subtract)
                done(pool.tensor_tensor(mo_dev[:], stats[:, :, 2:3], stats[:, :, 5:6], ALU.add))
                pool.tensor_tensor(mo_sq[:], mo_dif[:], mo_dif[:], ALU.mult)
                pool.tensor_scalar(mo_dev[:], mo_dev[:], 1.0 / P, EPS, ALU.mult, ALU.add)
                done(pool.tensor_scalar(mean[:], mo_sum[:], 0.5, 0.0, ALU.mult, ALU.add))
                done(pool.tensor_tensor(mo_sq[:], mo_sq[:], quarter1, ALU.mult))
                done(pool.tensor_tensor(mo_dev[:], mo_dev[:], mo_sq[:], ALU.add))
                pool.tensor_tensor(rstd[:], mo_dev[:], minus_half[:].unsqueeze(2), ALU.pow).then_inc(moment_chain, 1)

            moments(Step(0, 0))
            pool.wait_ge(s_vec, 16)
            pool.tensor_scalar(scale_c[:], vcol[:, V_V1:V_V2 + 1:4], 1.0, EPS, ALU.mult, ALU.add).then_inc(pool_pow, 1)
            pool.wait_ge(pool_pow, 1)
            pool.tensor_tensor(scale_c[:], scale_c[:], minus_half[:, 0:2], ALU.pow).then_inc(pool_pow, 1)
            pool.memset(factor[:].bitcast(f32), 0.0).then_inc(pool_pow, 1)
            pool.wait_ge(s_w2, 16)
            pool.tensor_tensor(sums(1), tap(0), tap(1), ALU.add)
            pool.tensor_tensor(sums(3), tap(0), tap(2), ALU.add)
            pool.tensor_tensor(sums(4), tap(1), tap(3), ALU.add).then_inc(pool_sums, 1)
            factors(Step(0, 0))
            moments(Step(0, 1))
            message_lo(Step(0, 0))
            pool.wait_ge(act_set, 3)
            pool.wait_ge(w2_done, 2)
            pool.tensor_tensor(w2_lo[:, TAPS:NW2], w2_raw[:, TAPS:NW2], w2_hi[:, TAPS:NW2].bitcast(f32),
                               ALU.subtract).then_inc(sum_lo, 1)

            def body(i, front, norm, far):
                if norm:
                    moments(i + 2)
                pool.wait_ge(ps_done, i.after(1, 1))
                past(pool, y_done, i.after(2, 0))
                for c in (1, 2):
                    pool.tensor_tensor(phases(xc, c), two(p_sum), phases(h[i.par()][:], c), ALU.add).then_inc(xs_done, 1)
                if front:
                    factors(i + 1)
                    message_lo(i + 1)
                for k in range(2 if front else 0):
                    pool.wait_ge(cand_done, i.after(2, k + 1))
                    past(pool, s_out[k], i.after(16, 0))
                    pool.tensor_tensor(dif[k], h[i.par()][:, halves(k)], cand[k], ALU.subtract).then_inc(dif_done, 1)
                    pool.wait_ge(upd_done, i.after(2, k + 1))
                    pool.wait_ge(s_res, i.after(16, 16))
                    pool.tensor_tensor(upd[k], upd[k], res[:, halves(k)], ALU.add).then_inc(y_done, 1)

            steps(pool, body)

        @block.scalar
        def _(act):
            def norm_evac(s):
                for k in range(2):
                    act.wait_ge(tr_done, s.after(2, k + 1))
                    act.activation(h[s.par()][:, halves(k)], bank[B_FRONT[k]][:], ACT.Relu)
                    act.activation(h_hi[s.par()][:, halves(k)], bank[B_FRONT[k]][:], ACT.Relu).then_inc(hh_done, 1)

            def conv1_evac(s):
                for k in range(2):
                    act.wait_ge(c1_mm, s.after(2, k + 1))
                    if k == 0:
                        past(act, ql_done, s.after(3, 0))
                        past(act, qh_done, s.after(3, 0))
                    act.activation(c1[:, 2 * k:2 * k + 2, PAD:PAD + N_NODE],
                                   bank[B_FRONT[k]][:].rearrange("p (b n) -> p b n", b=2), ACT.Relu,
                                   bias=bias_c[:, 0:1], scale=scale_c[:, 0:1]).then_inc(c1_act, 1)

            def msg_evac(s):
                for q, (t0, nt) in enumerate(MSG_LOTS):
                    act.wait_ge(ms_mm, s.after(3, q + 1))
                    v = bank[B_MSG[q]][:, 0:nt * MSGW].rearrange("p (t c) -> p t c", c=MSGW)
                    if q == 0:
                        past(act, factor_chain, s.after(PF, 0))
                        past(act, ml_done, s.after(1, 0))
                    act.activation(se[:, t0:t0 + nt, :], v[:, :, P:P + 3], ACT.Copy).then_inc(se_act, 1)
                    act.activation(msg[:, t0:t0 + nt, :], v[:, :, 0:P], ACT.Relu)
                    act.activation(msg_hi[:, t0:t0 + nt, :], v[:, :, 0:P], ACT.Relu).then_inc(ms_act, 1)

            def factor_copy(s):
                act.wait_ge(ft_done, s.after(1, 1))
                past(act, di_mm, s.after(STEP_B, 0))
                for q in (2, 3):
                    last = act.activation(factor_rows(q), feat_t[32 * q:32 * q + 16], ACT.Copy)
                last.then_inc(fc_act, 1)

            def affinity(s, b):
                act.wait_ge(di_mm, s.after(STEP_B, b + 1))
                if b >= 2:
                    act.wait_ge(aff_done, s.after(STEP_B, b - 1))
                act.activation(aff[:, b % 2, :], bank[B_DIST[b]][:], ACT.Exp).then_inc(exp_done, 1)

            def aff_hi_part(s, b):
                act.wait_ge(aff_done, s.after(STEP_B, b + 1))
                act.activation(aff_hi[:, b, :], mask[:, b, :], ACT.Copy).then_inc(afh_done, 1)

            def agg_evac(s):
                for k in range(2):
                    act.wait_ge(ag_mm, s.after(2, k + 1))
                    act.activation(agg_hi[:, halves(k)], bank[B_AGG[k]][:], ACT.Copy).then_inc(agh_done, 1)

            def quarter_hi(s, c):
                act.wait_ge(qd_done, s.after(3, c + 1))
                past(act, c2_mm, s.after(6, 2 * c - 4))
                act.activation(quart_hi[:, c, 0], odds(*half_seq(c), QROW), ACT.Copy)
                act.activation(flat(quart_hi[:, c, 1:3]), flat(quart_dif[:, c]),
                               ACT.Copy).then_inc(qh_done, 1)

            def pp_evac(i):
                act.wait_ge(c2_mm, i.after(6, 1))
                past(act, ps_done, i.after(1, 0))
                act.wait_ge(w_ready, 4)
                act.activation(pp, bank[B_PP][:, 0:HALF // 2], ACT.Copy, scale=scale_c[:, 1:2]).then_inc(pp_act, 1)

            def conv2_relu(i, k):
                act.wait_ge(yc_done, i.after(3, k + 2))
                act.activation(xc[:, halves(k)], xc[:, halves(k)], ACT.Relu, bias=bias_c[:, 1:2]).then_inc(xc_done, 1)

            def hidden_n(i, k):
                act.wait_ge(gn_mm, i.after(2, k + 1))
                past(act, upd_done, i.after(2, 0))
                act.activation(ghn[k], bank[B_GN][:], ACT.Identity, bias=bias_c[:, 5:6], scale=0.5).then_inc(gn_act, 1)

            def gate_tanh(i, k):
                act.wait_ge(g_mm, i.after(6, 3 * k + 1))
                act.activation(tr[k], bank[B_R][:], ACT.Tanh, bias=bias_c[:, 2:3], scale=0.5).then_inc(tr_act, 1)
                act.wait_ge(g_mm, i.after(6, 3 * k + 2))
                act.activation(tz[k], bank[B_Z][:], ACT.Tanh, bias=bias_c[:, 3:4], scale=0.5).then_inc(tz_act, 1)

            def cand_tanh(i, k):
                act.wait_ge(pre_done, i.after(2, k + 1))
                act.activation(cand[k], pre[k], ACT.Tanh, bias=bias_c[:, 4:5]).then_inc(cand_done, 1)

            z = Step(0, 0)
            act.wait_ge(s_w1, 16)
            act.activation(w1_hi[:], w1_raw, ACT.Copy).then_inc(act_set, 1)
            norm_evac(z)
            act.wait_ge(s_w2, 16)
            act.activation(w2_hi[:, 0:TAPS], w2_raw[:, 0:TAPS], ACT.Copy).then_inc(act_set, 1)
            msg_evac(z)
            act.wait_ge(dve_set, 5)
            conv1_evac(z)
            act.wait_ge(w2_done, 2)
            act.activation(w2_hi[:, TAPS:NW2], w2_raw[:, TAPS:NW2], ACT.Copy).then_inc(act_set, 1)
            quarter_hi(z, 0)
            act.wait_ge(pool_pow, 3)
            factor_copy(z)
            quarter_hi(z, 1)
            quarter_hi(z, 2)
            for b in range(STEP_B):
                affinity(z, b)
            for b in range(STEP_B):
                aff_hi_part(z, b)
            act.wait_ge(s_wg, 16)
            act.activation(wg_hi[:], wg_raw, ACT.Copy).then_inc(act_set, 1)
            agg_evac(z)

            def body(i, front, norm, far):
                if front:
                    past(act, dif_done, i.after(2, 0))
                    norm_evac(i + 1)
                pp_evac(i)
                if front:
                    conv1_evac(i + 1)
                    msg_evac(i + 1)
                    quarter_hi(i + 1, 0)
                    quarter_hi(i + 1, 1)
                    factor_copy(i + 1)
                conv2_relu(i, 0)
                conv2_relu(i, 1)
                hidden_n(i, 0)
                if front:
                    quarter_hi(i + 1, 2)
                gate_tanh(i, 0)
                if front:
                    affinity(i + 1, 0)
                    affinity(i + 1, 1)
                cand_tanh(i, 0)
                if front:
                    affinity(i + 1, 2)
                    aff_hi_part(i + 1, 0)
                    affinity(i + 1, 3)
                    aff_hi_part(i + 1, 1)
                    aff_hi_part(i + 1, 2)
                hidden_n(i, 1)
                gate_tanh(i, 1)
                if front:
                    aff_hi_part(i + 1, 3)
                cand_tanh(i, 1)
                if front:
                    agg_evac(i + 1)

            steps(act, body)

        @block.vector
        def _(dve):
            chain = [0]

            def link(ins):
                chain[0] += 1
                ins.then_inc(dve_set, 1)
                dve.wait_ge(dve_set, chain[0])

            def norm_stats(s):
                dve.wait_ge(s_x[s.par()], s.load())
                past(dve, moment_chain, s.after(PM, 0))
                for t in range(TILES):
                    last = dve.bn_stats(stats[:, t, :], xt[s.par()][:, t, :])
                last.then_inc(st_done, 1)

            def norm_apply(s):
                dve.wait_ge(moment_chain, s.after(PM, PM))
                for t in range(TILES):
                    last = dve.tensor_scalar(xt[s.par()][:, t, :], xt[s.par()][:, t, :], mean[:, t, :], rstd[:, t, :],
                                             ALU.subtract, ALU.mult)
                    if t % (TILES // 2) == TILES // 2 - 1:
                        last.then_inc(xn_done, 1)

            def norm_split(s):
                for k in range(2):
                    dve.wait_ge(hh_done, s.after(2, k + 1))
                    dve.tensor_tensor(h_lo[s.par()][:, halves(k)], h[s.par()][:, halves(k)],
                                      h_hi[s.par()][:, halves(k)].bitcast(f32), ALU.subtract).then_inc(hl_done, 1)

            def differences(s, cs):
                if 0 in cs:
                    dve.wait_ge(c1_act, s.after(2, 2))
                    past(dve, qh_done, s.after(3, 0))
                    dve.tensor_tensor(half_dif[:, :, :, 0:SROW - 1], evens(c1[:], 0, 1, SROW - 1),
                                      twice(odds(c1[:], 0, 1, SROW - 1)), ALU.subtract).then_inc(hd_done, 1)
                    dve.wait_ge(hd_done, s.after(1, 1))
                for c in cs:
                    dve.tensor_tensor(quart_dif[:, c], evens(*half_seq(c), QROW), twice(odds(*half_seq(c), QROW)),
                                      ALU.subtract).then_inc(qd_done, 1)

            def quarter_lo(s, c):
                dve.wait_ge(qh_done, s.after(3, c + 1))
                dve.tensor_tensor(quart_lo[:, c, 0], odds(*half_seq(c), QROW), quart_hi[:, c, 0].bitcast(f32), ALU.subtract)
                dve.tensor_tensor(flat(quart_lo[:, c, 1:3]), flat(quart_dif[:, c]), flat(quart_hi[:, c, 1:3]).bitcast(f32),
                                  ALU.subtract).then_inc(ql_done, 1)

            def factor_blocks(s):
                dve.wait_ge(factor_chain, s.after(PF, PF))
                past(dve, fc_act, s.after(1, 0))
                past(dve, fc_dve, s.after(1, 0))
                dve.transpose(feat_t.rearrange("p t s f -> p (t s f)"), feat[:].rearrange("p t s f -> p (t s f)"))\
                    .then_inc(ft_done, 1)
                dve.wait_ge(ft_done, s.after(1, 1))
                past(dve, di_mm, s.after(STEP_B, 0))
                for q in (0, 1):
                    last = dve.tensor_copy(factor_rows(q), feat_t[32 * q:32 * q + 16])
                last.then_inc(fc_dve, 1)

            def own_p(c):
                at = (c % 2) * (HALF // 2)
                return twice(bank[B_PP][:, at:at + HALF // 2])

            def p_combine(i):
                dve.wait_ge(pp_act, i.after(1, 1))
                dve.wait_ge(c2_mm, i.after(6, 2))
                past(dve, xs_done, i.after(2, 0))
                dve.scalar_tensor_tensor(two(p_sum), two(bank[B_PR[0]][:]), scale_c[:, 1:2], twice(pp),
                                         ALU.mult, ALU.add).then_inc(ps_done, 1)

            def combine_own(i, c):
                dve.wait_ge(c2_mm, i.after(6, 2 * c + 1))
                dve.wait_ge(xs_done, i.after(2, c))
                dve.scalar_tensor_tensor(phases(xc, c), own_p(c), scale_c[:, 1:2], phases(xc, c),
                                         ALU.mult, ALU.add).then_inc(qs_done, 1)

            def combine(i, c):
                dve.wait_ge(c2_mm, i.after(6, 2 * c + 2))
                dve.wait_ge(qs_done, i.after(2, c))
                for at in ([slice(0, QB)], [slice(0, QB // 2), slice(QB // 2, QB)])[c - 1]:
                    dve.scalar_tensor_tensor(phases(xc, c)[:, :, at], two(bank[B_PR[c]][:])[:, :, at], scale_c[:, 1:2],
                                             phases(xc, c)[:, :, at], ALU.mult, ALU.add).then_inc(yc_done, 1)

            def masks(s, bs):
                dve.wait_ge(s_mask, s.after(16, 16))
                for b in bs:
                    dve.wait_ge(exp_done, s.after(STEP_B, b + 1))
                    dve.tensor_tensor(mask[:, b, :], aff[:, b % 2, :], mask[:, b, :], ALU.mult).then_inc(aff_done, 1)

            def aff_split(s, bs):
                for b in bs:
                    dve.wait_ge(afh_done, s.after(STEP_B, b + 1))
                    dve.tensor_tensor(aff_lo[:, b, :], mask[:, b, :], aff_hi[:, b, :].bitcast(f32),
                                      ALU.subtract).then_inc(afl_done, 1)

            def agg_split(s):
                for k in range(2):
                    dve.wait_ge(agh_done, s.after(2, k + 1))
                    dve.tensor_tensor(agg_lo[:, halves(k)], bank[B_AGG[k]][:], agg_hi[:, halves(k)].bitcast(f32),
                                      ALU.subtract).then_inc(agl_done, 1)

            def conv2_split(i, k):
                dve.wait_ge(xc_done, i.after(2, k + 1))
                dve.tensor_copy(xc_hi[:, halves(k)], xc[:, halves(k)]).then_inc(xch_done, 1)
                dve.wait_ge(xch_done, i.after(2, k + 1))
                dve.tensor_tensor(xc_lo[:, halves(k)], xc[:, halves(k)], xc_hi[:, halves(k)].bitcast(f32),
                                  ALU.subtract).then_inc(xcl_done, 1)

            def candidate(i, k):
                dve.wait_ge(tr_act, i.after(2, k + 1))
                dve.scalar_tensor_tensor(rg[k], tr[k], 1.0, ghn[k], ALU.add, ALU.mult).then_inc(rg_done, 1)
                dve.wait_ge(rg_done, i.after(2, k + 1))
                dve.wait_ge(g_mm, i.after(6, 3 * k + 3))
                dve.tensor_tensor(pre[k], rg[k], bank[B_IN][:], ALU.add).then_inc(pre_done, 1)

            def update(i, k):
                dve.wait_ge(dif_done, i.after(2, k + 1))
                dve.wait_ge(tz_act, i.after(2, k + 1))
                dve.scalar_tensor_tensor(zd[k], tz[k], 1.0, dif[k], ALU.add, ALU.mult).then_inc(zd_done, 1)
                dve.wait_ge(zd_done, i.after(2, k + 1))
                past(dve, y_done, i.after(2, 0))
                dve.scalar_tensor_tensor(upd[k], zd[k], 0.5, cand[k], ALU.mult, ALU.add).then_inc(upd_done, 1)

            def finish(i, k):
                dve.wait_ge(tz_act, i.after(2, k + 1))
                dve.wait_ge(s_out[k], i.after(16, 0))
                dve.scalar_tensor_tensor(dif[k], tz[k], 1.0, h[i.par()][:, halves(k)],
                                         ALU.add, ALU.mult).then_inc(zd_done, 1)
                dve.tensor_scalar(tz[k], tz[k], -0.5, 0.5, ALU.mult, ALU.add).then_inc(dif_done, 1)
                dve.wait_ge(s_res, i.after(16, 16))
                dve.wait_ge(zd_done, i.after(2, k + 1))
                dve.scalar_tensor_tensor(dif[k], dif[k], 0.5, res[:, halves(k)], ALU.mult, ALU.add).then_inc(upd_done, 1)
                dve.wait_ge(cand_done, i.after(2, k + 1))
                dve.wait_ge(dif_done, i.after(2, k + 1))
                dve.tensor_tensor(cand[k], tz[k], cand[k], ALU.mult).then_inc(fin_done, 1)
                dve.wait_ge(fin_done, k + 1)
                dve.wait_ge(upd_done, i.after(2, k + 1))
                dve.tensor_tensor(upd[k], cand[k], dif[k], ALU.add).then_inc(y_done, 1)

            z = Step(0, 0)
            dve.memset(ones[:].bitcast(f32), 1.0)
            dve.memset(bias_msg[:].bitcast(f32), 0.0)
            dve.memset(c1[:], 0.0).then_inc(dve_fill, 1)
            norm_stats(z)
            dve.wait_ge(act_set, 1)
            dve.tensor_tensor(w1_lo[:], w1_raw, w1_hi[:].bitcast(f32), ALU.subtract).then_inc(w_ready, 1)
            dve.wait_ge(s_row, 16)
            dve.tensor_copy(mrow_hi, mrow[:]).then_inc(dve_fill, 1)
            dve.wait_ge(dve_fill, 2)
            for t in range(3):
                at = slice(t * MSGW, (t + 1) * MSGW)
                dve.tensor_copy(bias_msg[0:1, at], mrow_hi[0:1, :].bitcast(f32))
                last = dve.tensor_tensor(bias_msg[32:33, at], mrow[32:33, :], mrow_hi[32:33, :].bitcast(f32),
                                         ALU.subtract)
            last.then_inc(w_ready, 1)
            norm_apply(z)
            dve.wait_ge(s_vec, 16)
            dve.wait_ge(pool_pow, 2)
            link(dve.tensor_tensor(scale_c[:], scale_c[:], vcol[:, V_G1:V_G2 + 1:4], ALU.mult))
            link(dve.tensor_tensor(tmp_c[:], scale_c[:], vcol[:, V_M1:V_M2 + 1:4], ALU.mult))
            link(dve.tensor_tensor(bias_c[:, 0:2], vcol[:, V_B1:V_B2 + 1:4], tmp_c[:], ALU.subtract))
            link(dve.tensor_tensor(bias_c[:, 2:4], vcol[:, V_IR:V_IZ + 1], vcol[:, V_HR:V_HZ + 1], ALU.add))
            dve.tensor_copy(bias_c[:, 4:5], vcol[:, V_IN:V_IN + 1])
            dve.tensor_scalar(bias_c[:, 5:6], vcol[:, V_HN:V_HN + 1], 0.5, None, ALU.mult)
            link(dve.tensor_scalar(bias_c[:, 2:4], bias_c[:, 2:4], 0.5, None, ALU.mult))
            dve.wait_ge(s_w2, 16)
            dve.tensor_tensor(sums(2), tap(2), tap(3), ALU.add).then_inc(w2_done, 1)
            norm_split(z)
            norm_stats(z + 1)
            dve.wait_ge(w2_done, 1)
            dve.wait_ge(pool_sums, 1)
            dve.tensor_tensor(sums(0), sums(1), sums(2), ALU.add).then_inc(w2_done, 1)
            dve.wait_ge(act_set, 2)
            dve.tensor_tensor(w2_lo[:, 0:TAPS], w2_raw[:, 0:TAPS], w2_hi[:, 0:TAPS].bitcast(f32),
                              ALU.subtract).then_inc(w_ready, 1)
            differences(z, (0,))
            dve.wait_ge(pool_pow, 3)
            factor_blocks(z)
            differences(z, (1, 2))
            quarter_lo(z, 0)
            masks(z, range(STEP_B))
            aff_split(z, range(STEP_B))
            norm_apply(z + 1)
            quarter_lo(z, 1)
            quarter_lo(z, 2)
            dve.wait_ge(act_set, 4)
            dve.tensor_tensor(wg_lo[:], wg_raw, wg_hi[:].bitcast(f32), ALU.subtract).then_inc(w_ready, 1)
            norm_stats(z + 2)

            def body(i, front, norm, far):
                if front:
                    norm_split(i + 1)
                agg_split(i)
                p_combine(i)
                if norm:
                    norm_apply(i + 2)
                combine_own(i, 1)
                if front:
                    differences(i + 1, (0, 1, 2))
                combine(i, 1)
                if front:
                    factor_blocks(i + 1)
                combine_own(i, 2)
                if front:
                    quarter_lo(i + 1, 0)
                combine(i, 2)
                if front:
                    quarter_lo(i + 1, 1)
                conv2_split(i, 0)
                conv2_split(i, 1)
                if front:
                    quarter_lo(i + 1, 2)
                candidate(i, 0)
                if front:
                    masks(i + 1, (0, 1, 2))
                    aff_split(i + 1, (0,))
                    masks(i + 1, (3,))
                    aff_split(i + 1, (1, 2))
                    update(i, 0)
                    aff_split(i + 1, (3,))
                    candidate(i, 1)
                    if far:
                        norm_stats(i + 3)
                    update(i, 1)
                else:
                    finish(i, 0)
                    candidate(i, 1)
                    finish(i, 1)

            steps(dve, body)

        @block.tensor
        def _(pe):
            def mm(out_, w, x, start, stop):
                return pe.matmul(out_, w, x, start=start, stop=stop)

            def products(terms):
                return [(w, x) for (wh, wl), (xh, xl) in terms for w, x in ((wh, xh), (wh, xl), (wl, xh))]

            def group(out_, terms):
                pairs = products(terms)
                for q, (w, x) in enumerate(pairs):
                    last = mm(out_, w, x, q == 0, q == len(pairs) - 1)
                return last

            def transpose_x(s):
                for k in range(2):
                    pe.wait_ge(xn_done, s.after(2, k + 1))
                    for t in range(TILES // 2):
                        last = pe.transpose(bank[B_FRONT[k]][:, t * P:(t + 1) * P],
                                            xt[s.par()][:, k * TILES // 2 + t, :], ident[:])
                    last.then_inc(tr_done, 1)

            def conv1(s):
                p = s.par()
                pe.wait_ge(hl_done, s.after(2, 2))
                for k in range(2):
                    group(bank[B_FRONT[k]][:], [((w1_hi[:], w1_lo[:]), (h_hi[p][:, halves(k)], h_lo[p][:, halves(k)]))])\
                        .then_inc(c1_mm, 1)

            def messages(s):
                for q, (t0, nt) in enumerate(MSG_LOTS):
                    mm(bank[B_MSG[q]][:, 0:nt * MSGW], ones[:], bias_msg[:, 0:nt * MSGW], True, False)
                    for t in range(nt):
                        last = mm(bank[B_MSG[q]][:, t * MSGW:(t + 1) * MSGW], h[s.par()][:, (t0 + t) * P:(t0 + t + 1) * P],
                                  wm_sb[:], False, t == nt - 1)
                    last.then_inc(ms_mm, 1)

            def distances(s):
                pe.wait_ge(fc_act, s.after(1, 1))
                pe.wait_ge(fc_dve, s.after(1, 1))
                for b in range(STEP_B):
                    for m in range(MT):
                        at = b * N_NODE
                        last = mm(bank[B_DIST[b]][:, m * N_NODE:(m + 1) * N_NODE],
                                  factor[:, 0, at + m * P:at + (m + 1) * P], factor[:, 1, at:at + N_NODE], True, True)
                    last.then_inc(di_mm, 1)

            def aggregate(s, before=None):
                pe.wait_ge(exp_done, s.after(STEP_B, STEP_B))
                pe.wait_ge(ml_done, s.after(1, 1))
                for b in range(STEP_B):
                    if b == 2 and before:
                        pe.wait_ge(tz_act, before.after(2, 2))
                    pe.wait_ge(afl_done, s.after(STEP_B, b + 1))
                    o = bank[B_AGG[b // 2]][:, (b % 2) * N_NODE:(b % 2 + 1) * N_NODE]
                    last = group(o, [((msg_hi[:, t, :], msg_lo[:, t, :]), (aff_hi[:, b, at], aff_lo[:, b, at]))
                                     for t, at in ((b * MT + m, slice(m * N_NODE, (m + 1) * N_NODE)) for m in range(MT))])
                    if b % 2:
                        last.then_inc(ag_mm, 1)

            def weights(c, d, t):
                at = {(0, 0): TAPS, (0, 1): TAPS + 4, (0, 2): TAPS + 8, (1, 0): TAPS + 12, (2, 0): TAPS + 16}.get((c, d))
                if t == 4:
                    at = TAPS - 1
                elif at is None:
                    at = 4 * t + (c - 1) + 2 * (d - 1)
                else:
                    at += t
                return w2_hi[:, at, :], w2_lo[:, at, :]

            def wide(c, d):
                if d:
                    o = bank[B_PR[c]][:, (d - 1) * HALF // 2:d * HALF // 2]
                else:
                    o = bank[B_PP][:, (c % 2) * HALF // 2:(c % 2 + 1) * HALF // 2]
                taps = range(5 if c < 2 and d < 2 else 4)
                return group(o.rearrange("p (b v) -> p b v", b=STEP_B),
                             [(weights(c, d, t), (quart_hi[:, c, d, :, t:t + QN], quart_lo[:, c, d, :, t:t + QN]))
                              for t in taps])

            def conv2_p(i):
                pe.wait_ge(ql_done, i.after(3, 3))
                pe.wait_ge(exp_done, i.after(STEP_B, STEP_B))
                wide(0, 0).then_inc(c2_mm, 1)
                wide(0, 1)
                wide(0, 2).then_inc(c2_mm, 1)

            def conv2_q(i):
                pe.wait_ge(pp_act, i.after(1, 1))
                wide(1, 0).then_inc(c2_mm, 1)
                wide(1, 1)
                wide(1, 2).then_inc(c2_mm, 1)

            def conv2_r(i):
                pe.wait_ge(qs_done, i.after(2, 1))
                wide(2, 0).then_inc(c2_mm, 1)
                pe.wait_ge(ps_done, i.after(1, 1))
                wide(2, 1)
                wide(2, 2).then_inc(c2_mm, 1)

            def part(b, terms, first, last_):
                pairs = products(terms)
                for q, (w, x) in enumerate(pairs):
                    last = mm(bank[b][:], w, x, first and q == 0, last_ and q == len(pairs) - 1)
                return last

            def gates(i, k, front):
                p = i.par()
                hid = (h_hi[p][:, halves(k)], h_lo[p][:, halves(k)])
                con = (xc_hi[:, halves(k)], xc_lo[:, halves(k)])
                agg = (agg_hi[:, halves(k)], agg_lo[:, halves(k)])

                def w(src, gate):
                    return wg_hi[:, src, gate * P:(gate + 1) * P], wg_lo[:, src, gate * P:(gate + 1) * P]
                if k:
                    pe.wait_ge(tr_act, i.after(2, 1))
                else:
                    pe.wait_ge(w_ready, 4)
                part(B_R, [(w(0, 0), hid), (w(2, 0), agg)], True, False)
                if k:
                    pe.wait_ge(tz_act, i.after(2, 1))
                part(B_Z, [(w(0, 1), hid), (w(2, 1), agg)], True, False)
                if k:
                    pe.wait_ge(gn_act, i.after(2, 1))
                part(B_GN, [(w(0, 2), hid)], True, True).then_inc(gn_mm, 1)
                if k:
                    pe.wait_ge(pre_done, i.after(2, 1))
                else:
                    past(pe, pre_done, i.after(2, 0))
                part(B_IN, [(w(2, 2), agg)], True, False)
                if k == 0 and front:
                    pe.wait_ge(yc_done, i.after(3, 3))
                    distances(i + 1)
                pe.wait_ge(xcl_done, i.after(2, k + 1))
                part(B_R, [(w(1, 0), con)], False, True).then_inc(g_mm, 1)
                part(B_Z, [(w(1, 1), con)], False, True).then_inc(g_mm, 1)
                part(B_IN, [(w(1, 2), con)], False, True).then_inc(g_mm, 1)

            z = Step(0, 0)
            pe.wait_ge(pool_set, 3)
            transpose_x(z)
            pe.wait_ge(s_wm, 16)
            pe.wait_ge(w_ready, 2)
            pe.wait_ge(hh_done, 2)
            messages(z)
            conv1(z)
            pe.wait_ge(c1_act, z.after(2, 2))
            distances(z)
            aggregate(z)
            pe.wait_ge(w_ready, 3)
            pe.wait_ge(sum_lo, 1)

            def body(i, front, norm, far):
                if front:
                    transpose_x(i + 1)
                conv2_p(i)
                if front:
                    conv1(i + 1)
                    past(pe, pre_done, i.after(2, 0))
                    pe.wait_ge(agl_done, i.after(2, 2))
                    messages(i + 1)
                    pe.wait_ge(c1_act, (i + 1).after(2, 2))
                conv2_q(i)
                conv2_r(i)
                pe.wait_ge(agl_done, i.after(2, 2))
                if front:
                    pe.wait_ge(ms_act, (i + 1).after(3, 3))
                gates(i, 0, front)
                gates(i, 1, front)
                if front:
                    pe.wait_ge(tr_act, i.after(2, 2))
                    aggregate(i + 1, i)

            steps(pe, body)


_VECTORS = ["bn1_g", "bn1_b", "bn1_m", "bn1_v", "bn2_g", "bn2_b", "bn2_m", "bn2_v"]


def kernel(**inputs):
    import numpy as np
    import concourse.bacc as bacc
    from concourse import mybir
    from concourse.bass_utils import run_bass_kernel_spmd

    a = {k.replace("L0_gnn_", ""): np.asarray(v) for k, v in inputs.items()}
    x, adj = a["x"], a["adj"]
    vectors = np.concatenate([np.stack([a[n] for n in _VECTORS]), a["b_ih"].reshape(3, P), a["b_hh"].reshape(3, P)])
    w_ih, w_hh = a["w_ih"], a["w_hh"]
    arrays = {
        "x_tok": x.reshape(STEPS, TILES, P, P).transpose(0, 2, 1, 3),
        "x_chan": x.reshape(STEPS, STEP_TOK, P).transpose(0, 2, 1),
        "mask_t": adj.transpose(0, 2, 1).reshape(STEPS, STEP_B, MT, P, N_NODE).transpose(0, 3, 1, 2, 4)
                     .reshape(STEPS, P, STEP_B, HALF),
        "vec_col": vectors.T,
        "msg_row": np.concatenate([a["b_msg"], a["b_se"], np.zeros(1, np.float32)]).reshape(1, MSGW),
        "w1": a["conv1_w"][:, :, 0].T,
        "w2": a["conv2_w"].transpose(1, 2, 0),
        "wg": np.stack([w_hh.T, w_ih[:, :P].T, w_ih[:, P:].T], axis=1),
        "wm": np.concatenate([a["w_msg"].T, a["w_se"].T, np.zeros((P, 1), np.float32)], axis=1),
    }
    arrays = {k: np.ascontiguousarray(v) for k, v in arrays.items()}
    nc = bacc.Bacc("TRN2", target_bir_lowering=False, num_devices=1)
    args = [nc.dram_tensor(n, v.shape, mybir.dt.from_np(v.dtype), kind="ExternalInput").ap() for n, v in arrays.items()]
    out = nc.dram_tensor("out", (STEPS, P, STEP_TOK), mybir.dt.float32, kind="ExternalOutput").ap()
    gnn_layer(nc, *args, out)
    r = run_bass_kernel_spmd(nc, [arrays], core_ids=[0])
    return r.results[0]["out"].transpose(0, 2, 1).reshape(N_BATCH, N_NODE, P)
```
